# Optimizing a Trainium2 kernel written in Bass

```python
import numpy as np
import jax
import jax.numpy as jnp

def _softmax(x, axis=-1):
    return jax.nn.softmax(x, axis=axis)

def _gelu(x):
    return jax.nn.gelu(x, approximate=True)

def _silu(x):
    return jax.nn.silu(x)

def _sigmoid(x):
    return jax.nn.sigmoid(x)

def _layernorm(x, axis=-1, eps=1e-05):
    m = jnp.mean(x, axis=axis, keepdims=True)
    v = jnp.var(x, axis=axis, keepdims=True)
    return (x - m) / jnp.sqrt(v + eps)

def _scatter_add(tgt, idx, src, axis=0):
    return tgt.at[idx].add(src)

def _segment_sum(src, seg, n):
    return jax.ops.segment_sum(src, seg, n)
kernel_name = 'mk_audio_tower_d2_tok_audfeat256_r4_de0bd9'

def setup_inputs(seed: int=0):
    np.random.seed(seed)
    _w = jnp.asarray

    def _rec_inputs():
        import jax
        import jax.numpy as jnp
        _rk = jax.random.key(seed)
        x = -5.07413e-05 + 0.999912 * jax.random.normal(jax.random.fold_in(_rk, 1), (16, 750, 64), jnp.float32)
        return x
    x = _rec_inputs()

    def _L0_tok_setup():
        import jax, jax.numpy as jnp
        from jax import lax
        import numpy as np
        B, T, C, K, STRIDE = (16, 4000, 64, 5, 2)
        EPS = 0.001
        key = jax.random.key(seed)
        k0, k1, k2, k3 = jax.random.split(key, 4)
        x = jax.random.normal(k0, (B, T, C), dtype=jnp.float32)
        w = jax.random.normal(k1, (K, 1, C), dtype=jnp.float32) * 0.1
        b = jax.random.normal(k2, (C,), dtype=jnp.float32) * 0.01
        gamma = jnp.ones((C,), dtype=jnp.float32)
        beta = jnp.zeros((C,), dtype=jnp.float32)
        alpha = jnp.full((C,), 0.25, dtype=jnp.float32) + 0.01 * jax.random.normal(k3, (C,), dtype=jnp.float32)
        return {'x': x, 'w': w, 'b': b, 'gamma': gamma, 'beta': beta, 'alpha': alpha}
    _L0_tok_all = _L0_tok_setup()
    _L0_tok_in = {k: v for k, v in _L0_tok_all.items() if k in ('w', 'b', 'gamma', 'beta', 'alpha')}
    del _L0_tok_all

    def _L0_attn_setup():
        import jax, jax.numpy as jnp
        import numpy as np
        key = jax.random.key(seed)
        ks = jax.random.split(key, 5)
        b, t, e, h = (8, 256, 64, 8)
        w = lambda k, shape: jax.random.normal(k, shape, dtype=jnp.float32) * 0.02
        return {'x': jax.random.normal(ks[0], (b, t, e), dtype=jnp.float32), 'Wq': w(ks[1], (e, e * h)), 'bq': jnp.zeros((e * h,), jnp.float32), 'Wk': w(ks[2], (e, e * h)), 'bk': jnp.zeros((e * h,), jnp.float32), 'Wv': w(ks[3], (e, e * h)), 'bv': jnp.zeros((e * h,), jnp.float32), 'Wu': w(ks[4], (e * h, e)), 'bu': jnp.zeros((e,), jnp.float32)}
    _L0_attn_all = _L0_attn_setup()
    _L0_attn_in = {k: v for k, v in _L0_attn_all.items() if k in ('Wq', 'bq', 'Wk', 'bk', 'Wv', 'bv', 'Wu', 'bu')}
    del _L0_attn_all

    def _L0_ffn_setup():
        import jax, jax.numpy as jnp
        import numpy as np
        DIM = 64
        HEADS = 8
        NUM_KEYS = 64
        NUM_KV = NUM_KEYS ** 2
        PK_TOPK = 16
        FINAL_TOPK = 16
        DIM_KEY = DIM // 2
        P = 2

        def _pk(x, Wq_pk, pk_keys):
            b, n, _ = x.shape
            q = (x @ Wq_pk).reshape(b, n, P, HEADS, DIM_KEY).transpose(2, 0, 1, 3, 4)
            sim = jnp.einsum('pbnhd,pkhd->pbnhk', q, pk_keys)
            scores, idx = jax.lax.top_k(sim, PK_TOPK)
            idx0 = idx[0]
            idx1 = idx[1] * NUM_KEYS
            index = (idx0[..., :, None] + idx1[..., None, :]).reshape(b, n, HEADS, PK_TOPK * PK_TOPK)
            score = (scores[0][..., :, None] + scores[1][..., None, :]).reshape(b, n, HEADS, PK_TOPK * PK_TOPK)
            final_scores, pk_idx = jax.lax.top_k(score, FINAL_TOPK)
            final_indices = jnp.take_along_axis(index, pk_idx, axis=-1)
            final_scores = jax.nn.softmax(final_scores, axis=-1)
            return (final_scores, final_indices)
        key = jax.random.key(seed)
        ks = jax.random.split(key, 7)
        b, n = (2, 256)
        std = 0.02
        x = jax.random.normal(ks[0], (b, n, DIM), dtype=jnp.float32)
        Wq_pk = jax.random.normal(ks[1], (DIM, P * HEADS * DIM_KEY), dtype=jnp.float32) * std
        pk_keys = jax.random.normal(ks[2], (P, NUM_KEYS, HEADS, DIM_KEY), dtype=jnp.float32) * std
        Wq = jax.random.normal(ks[3], (DIM, HEADS * DIM), dtype=jnp.float32) * std
        keys_table = jax.random.normal(ks[4], (NUM_KV * HEADS, DIM), dtype=jnp.float32) * std
        values_table = jax.random.normal(ks[5], (NUM_KV * HEADS, DIM), dtype=jnp.float32) * std
        Wo = jax.random.normal(ks[6], (DIM * HEADS, DIM), dtype=jnp.float32) * std
        return {'x': x, 'Wq_pk': Wq_pk, 'pk_keys': pk_keys, 'Wq': Wq, 'keys_table': keys_table, 'values_table': values_table, 'Wo': Wo}
    _L0_ffn_all = _L0_ffn_setup()
    _L0_ffn_in = {k: v for k, v in _L0_ffn_all.items() if k in ('Wq_pk', 'pk_keys', 'Wq', 'keys_table', 'values_table', 'Wo')}
    del _L0_ffn_all

    def _L1_attn_setup():
        import jax, jax.numpy as jnp
        import numpy as np
        A, Bc, Cc = (0.5, 1.0, 1.0)
        H = 8
        EPS = 1e-12

        def _normalize(t):
            n = jnp.linalg.norm(t, axis=-1, keepdims=True)
            return t / jnp.maximum(n, EPS)
        key = jax.random.key(seed)
        ks = jax.random.split(key, 5)
        B, N, C = (8, 512, 64)
        D = C // H
        x = jax.random.normal(ks[0], (B, N, C), dtype=jnp.float32)
        Wqkv = jax.random.normal(ks[1], (3 * H * D, C), dtype=jnp.float32) * 0.02
        bqkv = jnp.zeros((3 * H * D,), dtype=jnp.float32)
        Wproj = jax.random.normal(ks[2], (C, H * D), dtype=jnp.float32) * 0.02
        bproj = jnp.zeros((C,), dtype=jnp.float32)
        temperature = jnp.ones((1, H, 1, 1), dtype=jnp.float32)
        return {'x': x, 'Wqkv': Wqkv, 'bqkv': bqkv, 'Wproj': Wproj, 'bproj': bproj, 'temperature': temperature}
    _L1_attn_all = _L1_attn_setup()
    _L1_attn_in = {k: v for k, v in _L1_attn_all.items() if k in ('Wqkv', 'bqkv', 'Wproj', 'bproj', 'temperature')}
    del _L1_attn_all

    def _L1_ffn_setup():
        import jax, jax.numpy as jnp
        import numpy as np
        B, S, H, F, E, K = (8, 1024, 64, 128, 16, 2)
        EPS = 1e-05
        key = jax.random.key(seed)
        ks = jax.random.split(key, 9)
        sc = 0.02
        return {'x': jax.random.normal(ks[0], (B, S, H), dtype=jnp.float32), 'gate_w': jax.random.normal(ks[1], (H, E), dtype=jnp.float32) * sc, 'gate_b': jnp.zeros((E,), dtype=jnp.float32), 'w1': jax.random.normal(ks[2], (E, H, F), dtype=jnp.float32) * sc, 'b1': jnp.zeros((E, F), dtype=jnp.float32), 'w2': jax.random.normal(ks[3], (E, F, H), dtype=jnp.float32) * sc, 'b2': jnp.zeros((E, H), dtype=jnp.float32), 'gamma': jnp.ones((H,), dtype=jnp.float32), 'beta': jnp.zeros((H,), dtype=jnp.float32)}
    _L1_ffn_all = _L1_ffn_setup()
    _L1_ffn_in = {k: v for k, v in _L1_ffn_all.items() if k in ('gate_w', 'gate_b', 'w1', 'b1', 'w2', 'b2', 'gamma', 'beta')}
    del _L1_ffn_all
    return {'x': x, 'L0_tok_w': _L0_tok_in['w'], 'L0_tok_b': _L0_tok_in['b'], 'L0_tok_gamma': _L0_tok_in['gamma'], 'L0_tok_beta': _L0_tok_in['beta'], 'L0_tok_alpha': _L0_tok_in['alpha'], 'L0_attn_Wq': _L0_attn_in['Wq'], 'L0_attn_bq': _L0_attn_in['bq'], 'L0_attn_Wk': _L0_attn_in['Wk'], 'L0_attn_bk': _L0_attn_in['bk'], 'L0_attn_Wv': _L0_attn_in['Wv'], 'L0_attn_bv': _L0_attn_in['bv'], 'L0_attn_Wu': _L0_attn_in['Wu'], 'L0_attn_bu': _L0_attn_in['bu'], 'L0_ffn_Wq_pk': _L0_ffn_in['Wq_pk'], 'L0_ffn_pk_keys': _L0_ffn_in['pk_keys'], 'L0_ffn_Wq': _L0_ffn_in['Wq'], 'L0_ffn_keys_table': _L0_ffn_in['keys_table'], 'L0_ffn_values_table': _L0_ffn_in['values_table'], 'L0_ffn_Wo': _L0_ffn_in['Wo'], 'L1_attn_Wqkv': _L1_attn_in['Wqkv'], 'L1_attn_bqkv': _L1_attn_in['bqkv'], 'L1_attn_Wproj': _L1_attn_in['Wproj'], 'L1_attn_bproj': _L1_attn_in['bproj'], 'L1_attn_temperature': _L1_attn_in['temperature'], 'L1_ffn_gate_w': _L1_ffn_in['gate_w'], 'L1_ffn_gate_b': _L1_ffn_in['gate_b'], 'L1_ffn_w1': _L1_ffn_in['w1'], 'L1_ffn_b1': _L1_ffn_in['b1'], 'L1_ffn_w2': _L1_ffn_in['w2'], 'L1_ffn_b2': _L1_ffn_in['b2'], 'L1_ffn_gamma': _L1_ffn_in['gamma'], 'L1_ffn_beta': _L1_ffn_in['beta']}

def reference(x, L0_tok_w, L0_tok_b, L0_tok_gamma, L0_tok_beta, L0_tok_alpha, L0_attn_Wq, L0_attn_bq, L0_attn_Wk, L0_attn_bk, L0_attn_Wv, L0_attn_bv, L0_attn_Wu, L0_attn_bu, L0_ffn_Wq_pk, L0_ffn_pk_keys, L0_ffn_Wq, L0_ffn_keys_table, L0_ffn_values_table, L0_ffn_Wo, L1_attn_Wqkv, L1_attn_bqkv, L1_attn_Wproj, L1_attn_bproj, L1_attn_temperature, L1_ffn_gate_w, L1_ffn_gate_b, L1_ffn_w1, L1_ffn_b1, L1_ffn_w2, L1_ffn_b2, L1_ffn_gamma, L1_ffn_beta):
    import jax
    import jax.numpy as jnp

    def _L0_tok_ref(x, w, b, gamma, beta, alpha):
        import jax, jax.numpy as jnp
        from jax import lax
        import numpy as np
        B, T, C, K, STRIDE = (16, 4000, 64, 5, 2)
        EPS = 0.001
        y = lax.conv_general_dilated(x, w, window_strides=(STRIDE,), padding='SAME', dimension_numbers=('NWC', 'WIO', 'NWC'), feature_group_count=C) + b
        mean = jnp.mean(y, axis=(1, 2), keepdims=True)
        var = jnp.var(y, axis=(1, 2), keepdims=True)
        yn = (y - mean) * lax.rsqrt(var + EPS) * gamma + beta
        return jnp.where(yn > 0, yn, alpha * yn)

    def _L0_attn_ref(x, Wq, bq, Wk, bk, Wv, bv, Wu, bu):
        import jax, jax.numpy as jnp
        import numpy as np
        b, t, e = x.shape
        h = Wq.shape[1] // e
        q = (x @ Wq + bq).reshape(b, t, h, e)
        k = (x @ Wk + bk).reshape(b, t, h, e)
        v = (x @ Wv + bv).reshape(b, t, h, e)
        scores = jnp.einsum('bihe,bjhe->bhij', q, k) / jnp.sqrt(jnp.asarray(e, jnp.float32))
        i = jnp.arange(t)[:, None]
        j = jnp.arange(t)[None, :]
        scores = jnp.where(j >= i, -jnp.inf, scores)
        scores = jnp.where(i == 0, 0.0, scores)
        att = jax.nn.softmax(scores, axis=-1)
        att = jnp.where(i == 0, 0.0, att)
        out = jnp.einsum('bhij,bjhe->bihe', att, v).reshape(b, t, h * e)
        return out @ Wu + bu

    def _L0_ffn_ref(x, Wq_pk, pk_keys, Wq, keys_table, values_table, Wo):
        import jax, jax.numpy as jnp
        import numpy as np
        DIM = 64
        HEADS = 8
        NUM_KEYS = 64
        NUM_KV = NUM_KEYS ** 2
        PK_TOPK = 16
        FINAL_TOPK = 16
        DIM_KEY = DIM // 2
        P = 2

        def _pk(x, Wq_pk, pk_keys):
            b, n, _ = x.shape
            q = (x @ Wq_pk).reshape(b, n, P, HEADS, DIM_KEY).transpose(2, 0, 1, 3, 4)
            sim = jnp.einsum('pbnhd,pkhd->pbnhk', q, pk_keys)
            scores, idx = jax.lax.top_k(sim, PK_TOPK)
            idx0 = idx[0]
            idx1 = idx[1] * NUM_KEYS
            index = (idx0[..., :, None] + idx1[..., None, :]).reshape(b, n, HEADS, PK_TOPK * PK_TOPK)
            score = (scores[0][..., :, None] + scores[1][..., None, :]).reshape(b, n, HEADS, PK_TOPK * PK_TOPK)
            final_scores, pk_idx = jax.lax.top_k(score, FINAL_TOPK)
            final_indices = jnp.take_along_axis(index, pk_idx, axis=-1)
            final_scores = jax.nn.softmax(final_scores, axis=-1)
            return (final_scores, final_indices)
        b, n, d = x.shape
        q = (x @ Wq).reshape(b, n, HEADS, DIM) * DIM ** (-0.5)
        kv_scores, indices = _pk(x, Wq_pk, pk_keys)
        offsets = jnp.arange(HEADS, dtype=indices.dtype) * NUM_KV
        ind = indices + offsets[None, None, :, None]
        k = jnp.einsum('bnhk,bnhkd->bnhd', kv_scores, keys_table[ind])
        v = jnp.einsum('bnhk,bnhkd->bnhd', kv_scores, values_table[ind])
        sim = jnp.einsum('bihd,bjhd->bhij', q, k)
        neg = -jnp.finfo(sim.dtype).max
        causal = jnp.tril(jnp.ones((n, n), dtype=bool))
        sim = jnp.where(causal, sim, neg)
        attn = jax.nn.softmax(sim, axis=-1)
        out = jnp.einsum('bhij,bjhd->bhid', attn, v)
        out = out.transpose(0, 2, 1, 3).reshape(b, n, HEADS * DIM)
        return out @ Wo

    def _L1_attn_ref(x, Wqkv, bqkv, Wproj, bproj, temperature):
        import jax, jax.numpy as jnp
        import numpy as np
        A, Bc, Cc = (0.5, 1.0, 1.0)
        H = 8
        EPS = 1e-12

        def _normalize(t):
            n = jnp.linalg.norm(t, axis=-1, keepdims=True)
            return t / jnp.maximum(n, EPS)
        B, N, C = x.shape
        D = C // H
        scale = float(D) ** 0.25
        qkv = (x @ Wqkv.T + bqkv).reshape(B, N, 3, H, D)
        qkv = jnp.transpose(qkv, (2, 0, 3, 1, 4))
        q, k, v = (qkv[0], qkv[1], qkv[2])
        q = q * scale
        v1 = jnp.concatenate([jnp.ones((B, H, N, 1), dtype=v.dtype), v], axis=-1)
        qn = _normalize(q) * (scale * temperature)
        kn = _normalize(k) * scale
        vN = v1 / N
        kv_mod = jnp.einsum('bhni,bhnj,bhne->bhije', kn, kn, vN)
        kv = jnp.einsum('bhnd,bhne->bhde', kn, vN)
        vsum = jnp.sum(vN, axis=-2)[:, :, None, :]
        y = A * jnp.einsum('bhni,bhnj,bhije->bhne', qn, qn, kv_mod) + scale ** 2 * Bc * jnp.einsum('bhnd,bhde->bhne', qn, kv) + scale ** 4 * Cc * vsum
        y_norm, y = (y[..., :1], y[..., 1:])
        y = y / y_norm
        out = jnp.transpose(y, (0, 2, 1, 3)).reshape(B, N, H * D)
        return out @ Wproj.T + bproj

    def _L1_ffn_ref(x, gate_w, gate_b, w1, b1, w2, b2, gamma, beta):
        import jax, jax.numpy as jnp
        import numpy as np
        B, S, H, F, E, K = (8, 1024, 64, 128, 16, 2)
        EPS = 1e-05
        gate_logits = x @ gate_w + gate_b
        topk_vals, topk_idx = jax.lax.top_k(gate_logits, K)
        topk_w = jax.nn.softmax(topk_vals, axis=-1)
        h = jax.nn.relu(jnp.einsum('bsh,ehf->bsef', x, w1) + b1)
        expert_out = jnp.einsum('bsef,efh->bseh', h, w2) + b2
        sel = jnp.take_along_axis(expert_out, topk_idx[:, :, :, None], axis=2)
        moe = jnp.sum(topk_w[..., None] * sel, axis=2)
        y = x + moe
        mu = jnp.mean(y, axis=-1, keepdims=True)
        var = jnp.var(y, axis=-1, keepdims=True)
        return (y - mu) / jnp.sqrt(var + EPS) * gamma + beta
    h = _L0_tok_ref(x, L0_tok_w, L0_tok_b, L0_tok_gamma, L0_tok_beta, L0_tok_alpha)
    h = h + _L0_attn_ref(_layernorm(h, axis=-1), L0_attn_Wq, L0_attn_bq, L0_attn_Wk, L0_attn_bk, L0_attn_Wv, L0_attn_bv, L0_attn_Wu, L0_attn_bu)
    h = h + _L0_ffn_ref(_layernorm(h, axis=-1), L0_ffn_Wq_pk, L0_ffn_pk_keys, L0_ffn_Wq, L0_ffn_keys_table, L0_ffn_values_table, L0_ffn_Wo)
    h = h + _L1_attn_ref(_layernorm(h, axis=-1), L1_attn_Wqkv, L1_attn_bqkv, L1_attn_Wproj, L1_attn_bproj, L1_attn_temperature)
    h = h + _L1_ffn_ref(_layernorm(h, axis=-1), L1_ffn_gate_w, L1_ffn_gate_b, L1_ffn_w1, L1_ffn_b1, L1_ffn_w2, L1_ffn_b2, L1_ffn_gamma, L1_ffn_beta)
    return h

_drawn_inputs = setup_inputs


def setup_inputs(seed=0):
    import zlib

    import numpy as np

    out = dict(_drawn_inputs(seed))
    spreads = {'L0_tok_gamma': (1.0, 0.2),
     'L0_tok_beta': (0.0, 0.1),
     'L0_attn_bq': (0.0, 0.8),
     'L0_attn_bk': (0.0, 2.0),
     'L0_attn_bv': (0.0, 0.1),
     'L0_attn_bu': (0.0, 0.1),
     'L1_attn_bqkv': (0.0, 0.302),
     'L1_attn_bproj': (0.0, 0.1),
     'L1_attn_temperature': (1.0, 0.6),
     'L1_ffn_gate_b': (0.0, 0.1),
     'L1_ffn_b1': (0.0, 0.8),
     'L1_ffn_b2': (0.0, 0.27),
     'L1_ffn_gamma': (1.0, 0.2),
     'L1_ffn_beta': (0.0, 0.1)}
    factors = {'L0_tok_alpha': 4.157,
     'L0_attn_Wq': 8.0,
     'L0_attn_Wk': 8.0,
     'L0_attn_Wv': 2.69,
     'L0_ffn_Wq_pk': 8.0,
     'L0_ffn_pk_keys': 8.0,
     'L0_ffn_Wq': 60.592,
     'L0_ffn_keys_table': 52.168,
     'L0_ffn_values_table': 8.0,
     'L0_ffn_Wo': 8.0,
     'L1_attn_Wqkv': 5.778,
     'L1_ffn_w1': 6.451,
     'L1_ffn_w2': 4.908}
    for name, (base, spread) in spreads.items():
        noise = np.random.default_rng([zlib.crc32(name.encode()), seed]).standard_normal(out[name].shape)
        drawn = base * np.exp(spread * noise) if base else spread * noise
        out[name] = jnp.asarray(drawn.astype(out[name].dtype))
    for name, factor in factors.items():
        out[name] = (out[name] * factor).astype(out[name].dtype)
    return out
```

```python
from contextlib import ExitStack

import concourse.bass as bass
from concourse import mybir

F32 = mybir.dt.float32
BF16 = mybir.dt.bfloat16
F16 = mybir.dt.float16
U32 = mybir.dt.uint32
ALU = mybir.AluOpType
ACT = mybir.ActivationFunctionType
AX = mybir.AxisListType

BATCH, T_IN, T, C = 16, 750, 375, 64
TAPS = 5
TP = 125
NT = T // TP
H, E = 8, 64
HE = H * E
PAIRS = H // 2
DK, NKEYS, TOPK = 32, 64, 16
GROUPS = 2 * H
CAND = [TOPK // (i + 1) for i in range(TOPK)]
NCAND = sum(CAND)
D1 = 8
PHI = D1 * D1 + D1 + 1
NEXP, F = 16, 128
N_LOADS = 30
RING = 6
BANKS = 4
MASKED = -1e30
KEY_BIAS = NKEYS * NKEYS // 2
EPS_CONV, EPS_LN, EPS_NORM = 1e-3, 1e-5, 1e-12
PER = {"act_filled": 155, "dve_filled": 30, "max_ready": 48, "kv_ready": 3, "indices_ready": 3,
       "xn_ready": 4, "var_ready": 7, "std_ready": 7, "o_ready": 6, "taps_done": 1, "conv_ready": 2,
       "exp_in": 4, "exp_out": 4, "phi_ready": 1, "gates_ready": 1, "y_ready": 1, "rows_used": 24,
       "kvm_ready": 1, "out_ready": 1, "x_loaded": 1, "values_moved": 1}


class Tally:

    def __init__(self):
        self.n, self.turn = {}, None

    def raised(self, name):
        self.n[name] = self.n.get(name, 0) + 1

    def value(self, name, k=None):
        k = self.n.get(name, 0) if k is None else k
        return k if self.turn is None else self.turn * PER[name] + k

    def loop(self, turn):
        self.turn, self.before = turn, dict(self.n)

    def end(self, turns):
        for name in self.n:
            per = self.n[name] - self.before.get(name, 0)
            assert per == PER[name], (name, per)
            self.n[name] += (turns - 1) * per
        self.turn = None


def build(nc, x, conv_w, conv_b, gamma0, beta0, alpha0, wq, bq, wk, bk, wv, bv, wu, bu,
          wpk_t, pk_keys_t, wq2, kv_table, wo, wqkv_t, bqkv, wproj_t, bproj, temperature,
          gate_w, gate_b, w1, b1, w2, b2, gamma1, beta1, out):
    with ExitStack() as ctx:
        def sb(name, shape, dtype=F32):
            return ctx.enter_context(nc.sbuf_tensor(name, shape, dtype))

        def sem(name):
            return ctx.enter_context(nc.semaphore(name))

        ident = sb("ident", [128, 128])
        identb = sb("identb", [128, 128], BF16)
        mask_strict = sb("mask_strict", [TP, TP], BF16)
        mask_causal = sb("mask_causal", [TP, TP], BF16)
        row_live = sb("row_live", [TP, 1])
        mean_of_c = sb("mean_of_c", [C, C])
        eps_conv = sb("eps_conv", [C, 1])
        eps_ln = sb("eps_ln", [TP, 1])
        iota = sb("iota", [TP, NEXP])
        iota_cand = sb("iota_cand", [TP, NCAND, H], F16)
        head_offset = sb("head_offset", [TP, H * TOPK])
        norm_in = sb("norm_in", [TP, 2 * H])
        norm_out = sb("norm_out", [TP, 2 * H])
        phi_coef = sb("phi_coef", [PHI, 1])
        taps_w = sb("taps_w", [C, TAPS])
        chan = sb("chan", [C, 4])
        Wq = sb("Wq", [C + 1, HE])
        Wk = sb("Wk", [C + 1, HE])
        Wv = sb("Wv", [C + 1, HE])
        Wu = sb("Wu", [128, PAIRS, C])
        Bu = sb("Bu", [C + 1, C])
        Wpk = sb("Wpk", [C, GROUPS * NKEYS])
        Wq2 = sb("Wq2", [C, HE])
        Wo = sb("Wo", [128, PAIRS, C])
        Wqkv = sb("Wqkv", [C + 1, 3 * C])
        Wproj = sb("Wproj", [C + 1, C])
        Wgate = sb("Wgate", [C + 1, NEXP])
        W1 = sb("W1", [C + 1, NEXP, F])
        W2 = sb("W2", [F, NEXP, C])
        B2 = sb("B2", [NEXP, C])
        Gamma1 = sb("Gamma1", [TP, C])
        Beta1 = sb("Beta1", [TP, C])

        xpad = sb("xpad", [C, T_IN + 4])
        conv = sb("conv", [C, T])
        conv_neg = sb("conv_neg", [C, T])
        cstat = sb("cstat", [C, 6])
        cmom = sb("cmom", [C, 2])
        call = sb("call", [C, 8])
        h_front = sb("h_front", [TP, NT, C])
        h_mid = sb("h_mid", [TP, NT, C])
        h_back = sb("h_back", [TP, NT, C])
        bstat = sb("bstat", [TP, NT, 6])
        bagg = sb("bagg", [TP, NT, 2])
        std = sb("std", [TP, NT])
        rstd = sb("rstd", [TP, NT])
        xn = sb("xn", [TP, NT, C])
        xn_moe = sb("xn_moe", [TP, NT, C])
        xT = [sb(f"xT{i}", [C + 1, T]) for i in range(5)]
        QKT = sb("QKT", [128, 2, PAIRS, T])
        QT, KT = QKT[:, 0, :, :], QKT[:, 1, :, :]
        Vbuf = sb("Vbuf", [TP, NT * H * PHI])
        V = Vbuf[:, 0:NT * HE].rearrange("p (t n) -> p t n", t=NT)
        negmax = sb("negmax", [TP, 4])
        sums = sb("sums", [TP, NT, H])
        rsum = sb("rsum", [TP, NT, H])
        probs = sb("probs", [TP, 2, T])
        probsT = sb("probsT", [TP, 2, T])
        O = sb("O", [TP, NT, HE])
        OTbuf = sb("OTbuf", [128, NT * H * PHI])
        OT = OTbuf[:, 0:NT * PAIRS * TP].rearrange("p (t n) -> p t n", t=NT)
        wide = sb("wide", [128, NEXP * T])
        scores = sb("scores", [TP, NT, GROUPS * NKEYS])
        top = sb("top", [TP, GROUPS, TOPK])
        top_at = sb("top_at", [TP, GROUPS, TOPK], U32)
        top_key = sb("top_key", [TP, GROUPS, TOPK])
        cand = sb("cand", [TP, H, NCAND])
        cand_key = sb("cand_key", [TP, NCAND, H], F16)
        best = sb("best", [TP, H, TOPK])
        best_at = sb("best_at", [TP, H, TOPK], U32)
        best_pos = sb("best_pos", [TP, TOPK, H], F16)
        onehot = wide[0:TP, 0:H * TOPK * NCAND // 2].bitcast(F16).rearrange("p (c k h) -> p c k h", c=NCAND, k=TOPK)
        below = sb("below", [TP, H, TOPK])
        expd = sb("expd", [TP, H, TOPK])
        esum = sb("esum", [TP, H])
        weight = sb("weight", [TP, NT, H, TOPK])
        index = sb("index", [128, NT, H * TOPK], U32)
        rows = sb("rows", [128, RING, TOPK, 2 * E])
        Wpk_t = rows[0:DK, 0, 0:8, :].rearrange("p k (n c) -> p (k n) c", c=C)
        Keys_t = rows[0:DK, 0, 8:16, :].rearrange("p k (n c) -> p (k n) c", c=NKEYS)
        KV = sb("KV", [TP, NT, 2, HE])
        odd = sb("odd", [TP, 2, E])
        QK = sb("QK", [TP, NT, 2 * H, D1])
        QKsq = sb("QKsq", [TP, NT, 2 * H, D1])
        V1 = sb("V1", [TP, NT, H, D1 + 1])
        nsq = sb("nsq", [TP, NT, 2 * H])
        nrm = sb("nrm", [TP, NT, 2 * H])
        phi_k = Vbuf[:, :].rearrange("p (t h f) -> p t h f", t=NT, h=H)
        phi_q = OTbuf[0:TP, :].rearrange("p (t h f) -> p t h f", t=NT, h=H)
        phi_qT = QKT[0:PHI, :, :, :].rearrange("p a g n -> p (a g n)").rearrange("p (t n) -> p t n", t=NT)
        KVM = sb("KVM", [PHI, H * (D1 + 1)])
        rden = sb("rden", [TP, NT, H])
        Y = sb("Y", [TP, NT, C])
        logits = sb("logits", [TP, NT, NEXP])
        lead = sb("lead", [TP, NT, 8])
        lead_at = sb("lead_at", [TP, NT, 8], U32)
        lead_pos = sb("lead_pos", [TP, NT, 8])
        ldiff = sb("ldiff", [TP, NT])
        lexp = sb("lexp", [TP, NT])
        gate1 = sb("gate1", [TP, NT])
        gate2 = sb("gate2", [TP, NT])
        gates = sb("gates", [TP, NT, NEXP])
        gates2 = sb("gates2", [TP, NT, NEXP])
        gatesT = sb("gatesT", [NEXP, T])
        hidden = wide[:, 0:NEXP * T].rearrange("p (e n) -> p e n", e=NEXP)
        weighed = O[:, 0:2, :].rearrange("p t (e c) -> p (t e) c", c=C)
        moe = sb("moe", [TP, NT, C])
        outb = sb("outb", [TP, NT, C])

        act_bank = [ctx.enter_context(nc.psum_tensor(f"act_bank{i}", [128, 512], F32)) for i in range(BANKS)]
        dve_bank = [ctx.enter_context(nc.psum_tensor(f"dve_bank{i}", [128, 512], F32)) for i in range(BANKS)]

        weights_loaded = sem("weights_loaded")
        consts_made = sem("consts_made")
        keys_folded = sem("keys_folded")
        dve_consts = sem("dve_consts")
        x_loaded = sem("x_loaded")
        out_stored = sem("out_stored")
        act_filled = sem("act_filled")
        act_drained = sem("act_drained")
        dve_filled = sem("dve_filled")
        dve_drained = sem("dve_drained")
        pool_passed = sem("pool_passed")
        pe_passed = sem("pe_passed")
        dve_step = sem("dve_step")
        sems = {n: sem(n) for n in PER if n not in ("act_filled", "dve_filled", "x_loaded")}
        sems.update(act_filled=act_filled, dve_filled=dve_filled)
        landed = [sem(f"rows_landed{i}") for i in range(RING)]

        block = ctx.enter_context(nc.Block())
        N_CONST, N_DVE_CONST = 18, 12

        def run(t, eng, start, iteration, finish):
            start()
            iteration(True, False)
            with eng.Fori(0, BATCH - 2) as turn:
                t.loop(turn)
                iteration(True, True)
                t.end(BATCH - 2)
            iteration(False, True)
            finish()

        @block.sync
        def _(sp):
            loads = [(taps_w[:, :], conv_w), (chan[:, 0:1], conv_b), (chan[:, 1:2], gamma0),
                     (chan[:, 2:3], beta0), (chan[:, 3:4], alpha0),
                     (Wq[0:C, :], wq), (Wq[C:C + 1, :], bq), (Wk[0:C, :], wk), (Wk[C:C + 1, :], bk),
                     (Wv[0:C, :], wv), (Wv[C:C + 1, :], bv), (Bu[C:C + 1, :], bu),
                     (Wu[:, :, :], wu.rearrange("(g p) c -> p g c", p=128)),
                     (Wpk_t[:, :, :], wpk_t), (Keys_t[:, :, :], pk_keys_t), (Wq2[:, :], wq2),
                     (Wo[:, :, :], wo.rearrange("(g p) c -> p g c", p=128)),
                     (Wqkv[0:C, :], wqkv_t), (Wqkv[C:C + 1, :], bqkv),
                     (Wproj[0:C, :], wproj_t), (Wproj[C:C + 1, :], bproj),
                     (norm_out[:, 0:H], temperature.broadcast_to([TP, H])),
                     (Wgate[0:C, :], gate_w), (Wgate[C:C + 1, :], gate_b),
                     (W1[0:C, :, :], w1.rearrange("e c f -> c e f")),
                     (W1[C:C + 1, :, :], b1.rearrange("(o e) f -> o e f", o=1)),
                     (W2[:, :, :], w2.rearrange("e f c -> f e c")), (B2[:, :], b2),
                     (Gamma1[:, :], gamma1.broadcast_to([TP, C])), (Beta1[:, :], beta1.broadcast_to([TP, C]))]
            assert len(loads) == N_LOADS
            sp.wait_ge(consts_made, N_CONST)
            sp.dma_start(xpad[:, 1:1 + T_IN], x[0]).then_inc(x_loaded, 16)
            for dst, src in loads:
                sp.dma_start(dst, src).then_inc(weights_loaded, 16)

            def load(b, n):
                sp.wait_ge(sems["taps_done"], n)
                sp.dma_start(xpad[:, 1:1 + T_IN], x[b]).then_inc(x_loaded, 16)

            def store(b, n):
                sp.wait_ge(sems["out_ready"], n)
                sp.dma_start(out[b].rearrange("(t p) c -> p t c", p=TP), outb[:, :, :]).then_inc(out_stored, 16)

            for b in (1, 2):
                load(b, b)
            with sp.Fori(0, BATCH - 3) as i:
                load(i + 3, i + 3)
                store(i, i + 1)
            for b in range(BATCH - 3, BATCH):
                store(b, b + 1)
            sp.wait_ge(out_stored, 16 * (BATCH + 1))

        @block.gpsimd
        def _(pool):
            done = [0]

            def made(ins):
                ins.then_inc(consts_made, 1)
                done[0] += 1

            for m in (ident, identb):
                made(pool.memset(m[:, :], 1.0))
            for m in (mask_strict, mask_causal):
                made(pool.memset(m[:, :], 0.0))
            made(pool.memset(row_live[:, :], 1.0))
            made(pool.iota(iota[:, :], [[1, NEXP]], base=0, channel_multiplier=0,
                           allow_small_or_imprecise_dtypes=True))
            made(pool.iota(iota_cand[:, :, :], [[1, NCAND], [0, H]], base=0, channel_multiplier=0,
                           allow_small_or_imprecise_dtypes=True))
            made(pool.iota(head_offset[:, :].rearrange("p (h k) -> p h k", h=H), [[NKEYS * NKEYS, H], [0, TOPK]],
                           base=KEY_BIAS, channel_multiplier=0, allow_small_or_imprecise_dtypes=True))
            made(pool.memset(index[:, :, :], 0))
            made(pool.memset(xpad[:, :], 0.0))
            made(pool.memset(phi_coef[:, :], D1 / T))
            pool.wait_ge(consts_made, done[0])
            for m in (ident, identb):
                made(pool.affine_select(out=m[:, :], in_=m[:, :], compare_op=ALU.is_equal, fill=0.0,
                                        base=0, pattern=[[-1, 128]], channel_multiplier=1))
            for m, first in ((mask_strict, -1), (mask_causal, 0)):
                made(pool.affine_select(out=m[:, :], in_=m[:, :], compare_op=ALU.is_ge, fill=MASKED,
                                        base=first, pattern=[[-1, TP]], channel_multiplier=1))
            made(pool.affine_select(out=row_live[:, :], in_=row_live[:, :], compare_op=ALU.is_gt, fill=0.0,
                                    base=0, pattern=[[0, 1]], channel_multiplier=1))
            made(pool.affine_select(out=phi_coef[:, :], in_=phi_coef[:, :], compare_op=ALU.is_ge,
                                    fill=float(D1) ** 0.5 / T, base=-(D1 * D1 + D1), pattern=[[0, 1]],
                                    channel_multiplier=1))
            pool.wait_ge(consts_made, done[0])
            made(pool.affine_select(out=phi_coef[:, :], in_=phi_coef[:, :], compare_op=ALU.is_ge,
                                    fill=0.5 / T, base=-D1 * D1, pattern=[[0, 1]], channel_multiplier=1))
            assert done[0] == N_CONST, done

            t = Tally()
            def gather(front, back):
                for tile in range(NT):
                    t.raised("indices_ready")
                    for h in range(H):
                        slot = (tile * H + h) % RING
                        if h == 0:
                            pool.wait_ge(sems["indices_ready"], t.value("indices_ready"))
                            pool.sem_inc(pool_passed, 1)
                        used = t.n.get("rows_used", 0) - RING + 1
                        if used > 0:
                            pool.wait_ge(sems["rows_used"], t.value("rows_used", used))
                            pool.sem_inc(pool_passed, 1)
                        t.raised("rows_used")
                        for k in range(TOPK):
                            at = h * TOPK + k
                            pool.indirect_dma_start(
                                rows[:, slot, k, :], None, kv_table,
                                bass.IndirectOffsetOnAxis(index[:, tile, at:at + 1], 0)).then_inc(landed[slot], 16)

            run(t, pool, lambda: None, gather, lambda: None)

        @block.tensor
        def _(pe):
            t = Tally()
            turn_base = {"act": 0, "dve": 0}

            def begin():
                turn_base["act"], turn_base["dve"] = t.n.get("act_filled", 0), t.n.get("dve_filled", 0)

            def bank(which):
                name = which + "_filled"
                n, base = t.n.get(name, 0), turn_base[which]
                free = max(n - BANKS + 1, base)
                if free > 0:
                    pe.wait_ge(act_drained if which == "act" else dve_drained, t.value(name, free))
                    pe.sem_inc(pe_passed, 1)
                return (act_bank if which == "act" else dve_bank)[(n - base) % BANKS]

            def full(which, ins):
                ins.then_inc(sems[which + "_filled"], 1)
                t.raised(which + "_filled")

            def drained(which, k=None):
                pe.wait_ge(act_drained if which == "act" else dve_drained, t.value(which + "_filled", k))
                pe.sem_inc(pe_passed, 1)

            def need(name):
                t.raised(name)
                pe.wait_ge(sems[name], t.value(name))
                pe.sem_inc(pe_passed, 1)

            def turn_tiles(src):
                b = bank("act")
                for i in range(NT):
                    ins = pe.transpose(b[0:C, i * TP:(i + 1) * TP], src[:, i, :], ident[0:TP, 0:TP])
                full("act", ins)

            def units(mask):
                for u in range(NT * H + 2):
                    if u < NT * H:
                        tile, h = divmod(u, H)
                        g, p = h // 2, 64 * (h % 2)
                        b = bank("act")
                        n = (tile + 1) * TP
                        pe.matmul(b[0:TP, 0:n], QT[p:p + E, g, tile * TP:n], KT[p:p + E, g, 0:n],
                                  start=True, stop=False)
                        full("act", pe.matmul(b[0:TP, n - TP:n], identb[0:TP, 0:TP], mask[:, :],
                                              start=False, stop=True))
                    if 1 <= u <= NT * H:
                        tile, h = divmod(u - 1, H)
                        b = bank("act")
                        drained("act", t.n["act_filled"] - (2 if 1 < u < NT * H else 1))
                        for j in range(tile + 1):
                            ins = pe.transpose(b[0:TP, j * TP:(j + 1) * TP],
                                               probs[:, (u - 1) % 2, j * TP:(j + 1) * TP], ident[0:TP, 0:TP])
                        full("act", ins)
                    if u >= 2:
                        tile, h = divmod(u - 2, H)
                        if h == 0:
                            units.ob = bank("dve")
                        drained("act", t.n["act_filled"] - (2 if u < NT * H else 1 if u == NT * H else 0))
                        for j in range(tile + 1):
                            ins = pe.matmul(units.ob[0:TP, h * E:(h + 1) * E],
                                            probsT[:, (u - 2) % 2, j * TP:(j + 1) * TP], V[:, j, h * E:(h + 1) * E],
                                            start=(j == 0), stop=(j == tile))
                        if h == H - 1:
                            full("dve", ins)

            def project(w, bias):
                for tile in range(NT):
                    need("o_ready")
                    b = bank("act")
                    for g in range(PAIRS):
                        ins = pe.transpose(b[:, g * TP:(g + 1) * TP], O[:, tile, g * 128:(g + 1) * 128],
                                           ident[0:TP, 0:TP])
                    full("act", ins)
                drained("act")
                for tile in range(NT):
                    b = bank("dve")
                    for g in range(PAIRS):
                        ins = pe.matmul(b[0:TP, 0:C], OT[:, tile, g * TP:(g + 1) * TP], w[:, g, :],
                                        start=(g == 0), stop=(g == PAIRS - 1 and not bias))
                    if bias:
                        ins = pe.matmul(b[0:TP, 0:C], xT[0][C:C + 1, tile * TP:(tile + 1) * TP],
                                        Bu[C:C + 1, :], start=False, stop=True)
                    full("dve", ins)

            def transposed_heads(w, k, src):
                for g in range(PAIRS):
                    full("act", pe.matmul(bank("act")[:, 0:T], w[0:k, g * 128:(g + 1) * 128], src[0:k, :],
                                          start=True, stop=True))

            def attention0():
                need("xn_ready")
                turn_tiles(xn)
                drained("act")
                transposed_heads(Wq, C + 1, xT[0])
                transposed_heads(Wk, C + 1, xT[0])
                for tile in range(NT):
                    full("act", pe.matmul(bank("act")[0:TP, :], xT[0][:, tile * TP:(tile + 1) * TP], Wv[:, :],
                                          start=True, stop=True))
                drained("act")
                units(mask_strict)
                project(Wu, True)

            def conv_stage():
                need("conv_ready")
                full("dve", pe.matmul(bank("dve")[0:C, 0:2], mean_of_c[:, :], cmom[:, :], start=True, stop=True))
                need("conv_ready")
                b = bank("dve")
                for i in range(NT):
                    ins = pe.transpose(b[0:TP, i * C:(i + 1) * C], conv[:, i * TP:(i + 1) * TP], ident[0:C, 0:C])
                full("dve", ins)

            def key_scores():
                need("xn_ready")
                turn_tiles(xn)
                drained("act")
                for tile in range(NT):
                    for half in range(2):
                        full("act", pe.matmul(bank("act")[0:TP, :], xT[1][0:C, tile * TP:(tile + 1) * TP],
                                              Wpk[:, half * 512:(half + 1) * 512], start=True, stop=True))

            def ffn_attention():
                transposed_heads(Wq2, C, xT[2])
                for g in range(PAIRS):
                    b = bank("act")
                    for i in range(NT):
                        ins = pe.transpose(b[:, i * TP:(i + 1) * TP], KV[:, i, 0, g * 128:(g + 1) * 128],
                                           ident[0:TP, 0:TP])
                    full("act", ins)
                drained("act")
                need("values_moved")
                units(mask_causal)
                project(Wo, False)

            def taylor_attention():
                need("xn_ready")
                turn_tiles(xn)
                drained("act")
                for i in range(NT):
                    full("dve", pe.matmul(bank("dve")[0:TP, 0:3 * C], xT[3][:, i * TP:(i + 1) * TP], Wqkv[:, :],
                                          start=True, stop=True))
                need("phi_ready")
                b = bank("dve")
                for h in range(H):
                    for i in range(NT):
                        ins = pe.matmul(b[0:PHI, h * 9:h * 9 + 9], phi_k[:, i, h, :], V1[:, i, h, :],
                                        start=(i == 0), stop=(i == NT - 1))
                full("dve", ins)
                for i in range(NT):
                    for half in range(2):
                        b = bank("act")
                        for j in range(4):
                            ins = pe.transpose(b[0:PHI, j * TP:(j + 1) * TP], phi_q[:, i, half * 4 + j, :],
                                               ident[0:TP, 0:TP])
                        full("act", ins)
                drained("act")
                need("kvm_ready")
                for i in range(NT):
                    b = bank("dve")
                    for h in range(H):
                        ins = pe.matmul(b[0:TP, h * 9:h * 9 + 9], phi_qT[:, i, h * TP:(h + 1) * TP],
                                        KVM[:, h * 9:h * 9 + 9], start=True, stop=True)
                    full("dve", ins)
                need("y_ready")
                turn_tiles(Y)
                drained("act")
                b = bank("dve")
                for i in range(NT):
                    ins = pe.matmul(b[0:TP, i * C:(i + 1) * C], xT[4][:, i * TP:(i + 1) * TP], Wproj[:, :],
                                    start=True, stop=True)
                full("dve", ins)

            def experts():
                need("xn_ready")
                turn_tiles(xn_moe)
                drained("act")
                b = bank("dve")
                for i in range(NT):
                    ins = pe.matmul(b[0:TP, i * NEXP:(i + 1) * NEXP], xT[3][:, i * TP:(i + 1) * TP],
                                    Wgate[:, :], start=True, stop=True)
                full("dve", ins)
                for e in range(NEXP):
                    full("act", pe.matmul(bank("act")[:, 0:T], W1[:, e, :], xT[3][:, :], start=True, stop=True))
                need("gates_ready")
                b = bank("act")
                for i in range(NT):
                    ins = pe.transpose(b[0:NEXP, i * TP:(i + 1) * TP], gates[:, i, :], ident[0:TP, 0:TP])
                full("act", ins)
                drained("act")
                for i in range(NT):
                    for half in range(2):
                        b = bank("dve")
                        for j in range(8):
                            e = half * 8 + j
                            ins = pe.matmul(b[0:TP, j * C:(j + 1) * C], hidden[:, e, i * TP:(i + 1) * TP],
                                            W2[:, e, :], start=True, stop=True)
                        full("dve", ins)
                b = bank("dve")
                for i in range(NT):
                    ins = pe.matmul(b[0:TP, i * C:(i + 1) * C], gatesT[:, i * TP:(i + 1) * TP], B2[:, :],
                                    start=True, stop=True)
                full("dve", ins)

            def start():
                pe.wait_ge(weights_loaded, 16 * N_LOADS)
                pe.wait_ge(consts_made, N_CONST)
                for g in range(GROUPS):
                    bk = act_bank[g // 8]
                    ins = pe.matmul(bk[0:C, (g % 8) * NKEYS:(g % 8 + 1) * NKEYS], Wpk_t[:, g, :], Keys_t[:, g, :],
                                    start=True, stop=True)
                ins.then_inc(keys_folded, 1)
                pe.wait_ge(keys_folded, 3)
                pe.wait_ge(dve_consts, N_DVE_CONST)
                conv_stage()
                attention0()
                key_scores()

            def iteration(front, back):
                begin()
                if back:
                    for i in range(NT):
                        need("kv_ready")
                    ffn_attention()
                if front:
                    conv_stage()
                    attention0()
                    key_scores()
                if back:
                    taylor_attention()
                    experts()

            def finish():
                begin()
                for i in range(NT):
                    need("kv_ready")
                ffn_attention()
                taylor_attention()
                experts()

            run(t, pe, start, iteration, finish)

        @block.scalar
        def _(act):
            t = Tally()
            base = [0]
            act.wait_ge(weights_loaded, 16 * N_LOADS)
            act.wait_ge(consts_made, N_CONST)

            def begin():
                base[0] = t.n.get("act_filled", 0)

            def take():
                k = t.n.get("act_filled", 0)
                t.raised("act_filled")
                act.wait_ge(act_filled, t.value("act_filled"))
                return act_bank[(k - base[0]) % BANKS]

            def copy_out(dst, src, func=ACT.Copy, scale=1.0):
                act.activation(dst, src, func, scale=scale).then_inc(act_drained, 1)

            def need(name):
                t.raised(name)
                act.wait_ge(sems[name], t.value(name))

            def std_of(dst, src, eps):
                need("var_ready")
                act.activation(dst, src, ACT.Sqrt, bias=eps).then_inc(sems["std_ready"], 1)

            def layer_norm():
                std_of(std[:, :], bagg[:, :, 1], eps_ln[:, 0:1])

            def exp_of(dst, src):
                need("exp_in")
                act.activation(dst, src, ACT.Exp).then_inc(sems["exp_out"], 1)

            def units():
                for u in range(NT * H + 1):
                    if u < NT * H:
                        tile, h = divmod(u, H)
                        n = (tile + 1) * TP
                        b = take()
                        need("max_ready")
                        act.activation(probs[:, u % 2, 0:n], b[0:TP, 0:n], ACT.Exp, bias=negmax[:, u % 4:u % 4 + 1],
                                       accum_out=sums[:, tile, h:h + 1]).then_inc(act_drained, 1)
                    if u >= 1:
                        n = ((u - 1) // H + 1) * TP
                        copy_out(probsT[:, (u - 1) % 2, 0:n], take()[0:TP, 0:n])

            def project():
                for tile in range(NT):
                    copy_out(OT[:, tile, :], take()[:, 0:PAIRS * TP])

            def attention0():
                layer_norm()
                copy_out(xT[0][0:C, :], take()[0:C, 0:T])
                for g in range(PAIRS):
                    copy_out(QT[:, g, :], take()[:, 0:T], scale=float(E) ** -0.5)
                for g in range(PAIRS):
                    copy_out(KT[:, g, :], take()[:, 0:T])
                for tile in range(NT):
                    copy_out(V[:, tile, :], take()[0:TP, :])
                units()
                project()

            def conv_stage():
                std_of(call[:, 3:4], call[:, 2:3], eps_conv[:, 0:1])

            def key_scores():
                layer_norm()
                b = take()
                copy_out(xT[1][0:C, :], b[0:C, 0:T])
                for tile in range(NT):
                    for half in range(2):
                        copy_out(scores[:, tile, half * 512:(half + 1) * 512], take()[0:TP, :])

            def key_exp():
                exp_of(expd[:, :, :], below[:, :, :])

            def ffn_attention():
                for i in range(NT):
                    need("kv_ready")
                act.activation(V, KV[:, :, 1, :], ACT.Copy).then_inc(sems["values_moved"], 1)
                for g in range(PAIRS):
                    copy_out(QT[:, g, :], take()[:, 0:T], scale=float(E) ** -0.5)
                for g in range(PAIRS):
                    copy_out(KT[:, g, :], take()[:, 0:T])
                units()
                project()

            def taylor_attention():
                layer_norm()
                copy_out(xT[3][0:C, :], take()[0:C, 0:T])
                need("var_ready")
                act.activation(nrm[:, :, :], nsq[:, :, :], ACT.Sqrt).then_inc(sems["std_ready"], 1)
                for i in range(NT):
                    for half in range(2):
                        copy_out(phi_qT[:, i, half * 4 * TP:(half + 1) * 4 * TP], take()[0:PHI, 0:4 * TP])
                copy_out(xT[4][0:C, :], take()[0:C, 0:T])

            def experts():
                layer_norm()
                copy_out(xT[3][0:C, :], take()[0:C, 0:T])
                for e in range(8):
                    copy_out(hidden[:, e, :], take()[:, 0:T], ACT.Relu)
                exp_of(lexp[:, :], ldiff[:, :])
                for e in range(8, NEXP):
                    copy_out(hidden[:, e, :], take()[:, 0:T], ACT.Relu)
                copy_out(gatesT[:, :], take()[0:NEXP, 0:T])
                layer_norm()

            def carry():
                act.activation(xT[2][0:C, :], xT[1][0:C, :], ACT.Copy)

            def start():
                act.wait_ge(keys_folded, 1)
                for half in range(2):
                    act.activation(Wpk[:, half * 512:(half + 1) * 512], act_bank[half][0:C, :],
                                   ACT.Copy).then_inc(keys_folded, 1)
                act.wait_ge(dve_consts, N_DVE_CONST)
                conv_stage()
                attention0()
                key_scores()
                for tile in range(NT):
                    key_exp()

            def iteration(front, back):
                begin()
                if back:
                    ffn_attention()
                carry()
                if front:
                    conv_stage()
                    attention0()
                    key_scores()
                    key_exp()
                if back:
                    taylor_attention()
                    experts()
                if front:
                    key_exp()
                    key_exp()

            def finish():
                begin()
                ffn_attention()
                taylor_attention()
                experts()

            run(t, act, start, iteration, finish)

        @block.vector
        def _(dve):
            t = Tally()
            base = [0]
            steps = [0]

            def step(ins):
                ins.then_inc(dve_step, 1)
                steps[0] += 1
                return steps[0]

            def after(k=None):
                dve.wait_ge(dve_step, steps[0] if k is None else k)

            def begin():
                base[0] = t.n.get("dve_filled", 0)

            def end():
                after()
                dve.sem_clear(dve_step)
                steps[0] = 0

            def take():
                k = t.n.get("dve_filled", 0)
                t.raised("dve_filled")
                dve.wait_ge(dve_filled, t.value("dve_filled"))
                return dve_bank[(k - base[0]) % BANKS]

            def drained():
                after()
                dve.sem_inc(dve_drained, 1)

            def signal(name):
                after()
                dve.sem_inc(sems[name], 1)

            def need(name):
                t.raised(name)
                dve.wait_ge(sems[name], t.value(name))

            def layer_stats(src):
                for i in range(NT):
                    step(dve.bn_stats(bstat[:, i, :], src[:, i, :]))
                for i in range(NT):
                    after(steps[0] - NT + 1)
                    step(dve.bn_aggr(bagg[:, i, :], bstat[:, i, :]))
                signal("var_ready")
                need("std_ready")
                step(dve.reciprocal(rstd[:, :], std[:, :]))
                after()

            def layer_norm(src, dst):
                layer_stats(src)
                for i in range(NT):
                    step(dve.tensor_scalar(dst[:, i, :], src[:, i, :], bagg[:, i, 0:1], rstd[:, i:i + 1],
                                           ALU.subtract, ALU.mult))
                signal("xn_ready")

            def softmax_units(strict, lots):
                for u in range(NT * H + 3):
                    if u < NT * H:
                        tile = u // H
                        t.raised("act_filled")
                        dve.wait_ge(act_filled, t.value("act_filled"))
                        if u >= 1:
                            t.raised("act_filled")
                        dve.tensor_reduce(negmax[:, u % 4:u % 4 + 1], softmax_units.bank(u)[0:TP, 0:(tile + 1) * TP],
                                          AX.X, ALU.max, negate=True).then_inc(sems["max_ready"], 1)
                        t.raised("max_ready")
                        sum_quarters(lots(u))
                    if u >= H + 2 and (u - 2) % H == 0:
                        tile = (u - 2) // H - 1
                        b = take()
                        step(dve.reciprocal(rsum[:, tile, :], sums[:, tile, :]))
                        after()
                        if strict and tile == 0:
                            step(dve.tensor_scalar(rsum[:, 0, :], rsum[:, 0, :], row_live[:, 0:1], None, ALU.mult))
                            after()
                        step(dve.tensor_tensor(
                            O[:, tile, :].rearrange("p (h e) -> p h e", h=H),
                            b[0:TP, :].rearrange("p (h e) -> p h e", h=H),
                            rsum[:, tile, :].unsqueeze(2).broadcast_to([TP, H, E]), ALU.mult))
                        drained()
                        dve.sem_inc(sems["o_ready"], 1)
                t.raised("act_filled")

            def add_projection(h):
                for _ in range(NT):
                    t.raised("act_filled")
                for i in range(NT):
                    b = take()
                    step(dve.tensor_tensor(h[:, i, :], h[:, i, :], b[0:TP, 0:C], ALU.add))
                    drained()

            def attention0(lots, fill=0):
                layer_norm(h_front, xn)
                sum_quarters(fill)
                for _ in range(1 + 2 * PAIRS + NT):
                    t.raised("act_filled")
                run_units(True, lots)
                add_projection(h_front)

            def run_units(strict, lots):
                first = t.n["act_filled"] - act_base[0]
                softmax_units.bank = lambda u: act_bank[(first + (2 * u - 1 if u else 0)) % BANKS]
                softmax_units(strict, lots)

            act_base = [0]

            def conv_stage():
                t.raised("x_loaded")
                dve.wait_ge(x_loaded, t.value("x_loaded") * 16)
                step(dve.tensor_scalar(conv[:, :], xpad[:, 0:2 * T:2], taps_w[:, 0:1], chan[:, 0:1],
                                       ALU.mult, ALU.add))
                for k in range(1, TAPS):
                    after()
                    step(dve.scalar_tensor_tensor(conv[:, :], xpad[:, k:k + 2 * T:2], taps_w[:, k:k + 1],
                                                  conv[:, :], ALU.mult, ALU.add))
                signal("taps_done")
                step(dve.bn_stats(cstat[:, :], conv[:, :]))
                after()
                step(dve.bn_aggr(cmom[:, :], cstat[:, :]))
                after()
                step(dve.scalar_tensor_tensor(cmom[:, 1:2], cmom[:, 0:1], cmom[:, 0:1], cmom[:, 1:2],
                                              ALU.mult, ALU.add))
                signal("conv_ready")
                b = take()
                step(dve.tensor_copy(call[:, 0:2], b[0:C, 0:2]))
                drained()
                step(dve.tensor_scalar(call[:, 4:5], call[:, 0:1], -1.0, None, ALU.mult))
                after()
                step(dve.scalar_tensor_tensor(call[:, 2:3], call[:, 4:5], call[:, 0:1], call[:, 1:2],
                                              ALU.mult, ALU.add))
                signal("var_ready")
                need("std_ready")
                step(dve.reciprocal(call[:, 5:6], call[:, 3:4]))
                after()
                step(dve.tensor_tensor(call[:, 6:7], call[:, 5:6], chan[:, 1:2], ALU.mult))
                after()
                step(dve.scalar_tensor_tensor(call[:, 7:8], call[:, 4:5], call[:, 6:7], chan[:, 2:3],
                                              ALU.mult, ALU.add))
                after()
                step(dve.tensor_scalar(conv[:, :], conv[:, :], call[:, 6:7], call[:, 7:8], ALU.mult, ALU.add))
                after()
                step(dve.tensor_scalar(conv_neg[:, :], conv[:, :], 0.0, chan[:, 3:4], ALU.min, ALU.mult))
                after()
                step(dve.scalar_tensor_tensor(conv[:, :], conv[:, :], 0.0, conv_neg[:, :], ALU.max, ALU.add))
                signal("conv_ready")
                b = take()
                step(dve.tensor_copy(h_front[:, :, :], b[0:TP, 0:NT * C].rearrange("p (t c) -> p t c", t=NT)))
                drained()

            def top16(count, best_of, at_of, src):
                for lot in range(2):
                    lo, hi = lot * 8, lot * 8 + 8
                    first = steps[0]
                    for g in range(count):
                        if lot:
                            after(first - count + 1 + g)
                        step(dve.max(best_of[:, g, lo:hi], src(g)))
                    for g in range(count):
                        after(first + 1 + g)
                        step(dve.max_index(at_of[:, g, lo:hi], best_of[:, g, lo:hi], src(g)))
                    if lot == 0:
                        for g in range(count):
                            step(dve.match_replace(src(g), best_of[:, g, lo:hi], src(g), -3.0e38))

            def key_norm():
                layer_norm(h_front, xn)

            def keys(tile):
                if tile == 0:
                    for _ in range(1 + 2 * NT):
                        t.raised("act_filled")
                dve.wait_ge(act_drained, t.value("act_filled", keys_filled[0] + 1 + 2 * (tile + 1)))
                dve.sem_inc(dve_step, 1)
                steps[0] += 1
                top16(GROUPS, top, top_at, lambda g: scores[:, tile, g * NKEYS:(g + 1) * NKEYS])
                after()
                step(dve.tensor_copy(top_key[:, 0:H, :], top_at[:, 0:H, :]))
                step(dve.tensor_scalar(top_key[:, H:, :], top_at[:, H:, :], float(NKEYS), -float(KEY_BIAS),
                                       ALU.mult, ALU.add))
                after()
                at, i = 0, 0
                while i < TOPK:
                    n = CAND[i]
                    m = CAND.count(n)
                    for dst, src in ((cand[:, :, at:at + m * n].rearrange("p h (i j) -> p h i j", i=m), top),
                                     (cand_key[:, at:at + m * n, :].rearrange("p (i j) h -> p h i j", i=m), top_key)):
                        step(dve.tensor_tensor(
                            dst, src[:, 0:H, i:i + m].unsqueeze(3).broadcast_to([TP, H, m, n]),
                            src[:, H:, 0:n].unsqueeze(2).broadcast_to([TP, H, m, n]), ALU.add))
                    at, i = at + m * n, i + m
                assert at == NCAND
                after()
                top16(H, best, best_at, lambda h: cand[:, h, :])
                after()
                step(dve.tensor_copy(best_pos[:, :, :], best_at[:, :, :].rearrange("p h k -> p k h")))
                step(dve.tensor_tensor(below[:, :, :], best[:, :, :],
                                       best[:, :, 0:1].broadcast_to([TP, H, TOPK]), ALU.subtract))
                signal("exp_in")
                flat = onehot.rearrange("p c k h -> p c (k h)")
                step(dve.tensor_tensor(onehot, iota_cand[:, :, :].unsqueeze(2).broadcast_to([TP, NCAND, TOPK, H]),
                                       best_pos[:, :, :].unsqueeze(1).broadcast_to([TP, NCAND, TOPK, H]),
                                       ALU.is_equal))
                after()
                step(dve.tensor_tensor(onehot, onehot, cand_key[:, :, :].unsqueeze(2)
                                       .broadcast_to([TP, NCAND, TOPK, H]), ALU.mult))
                n = NCAND
                while n > 1:
                    after()
                    half = n // 2
                    step(dve.tensor_tensor(flat[:, 0:half, :], flat[:, 0:half, :], flat[:, n - half:n, :], ALU.add))
                    n -= half
                after()
                step(dve.tensor_tensor(index[0:TP, tile, :].rearrange("p (h k) -> p h k", h=H),
                                       onehot[:, 0, :, :].rearrange("p k h -> p h k"),
                                       head_offset[:, :].rearrange("p (h k) -> p h k", h=H), ALU.add))
                need("exp_out")
                step(dve.tensor_reduce(esum[:, :], expd[:, :, :], AX.X, ALU.add))
                after()
                step(dve.reciprocal(esum[:, :], esum[:, :]))
                after()
                step(dve.tensor_tensor(weight[:, tile, :, :], expd[:, :, :],
                                       esum[:, :].unsqueeze(2).broadcast_to([TP, H, TOPK]), ALU.mult))
                signal("indices_ready")

            keys_filled = [0]

            summed = [0]

            def sum_quarters(count):
                for _ in range(count):
                    (tile, h), part = divmod(summed[0] // 4, H), summed[0] % 4
                    n = t.n.get("rows_used", 0)
                    slot = n % RING
                    kv = KV[:, tile, :, h * E:(h + 1) * E]
                    if part == 0:
                        arrived = 16 * TOPK * (n // RING + 1)
                        if t.turn is not None:
                            arrived = t.turn * (16 * TOPK * NT * H // RING) + arrived
                        dve.wait_ge(landed[slot], arrived)
                    for k in range(4 * part, 4 * part + 4):
                        row = rows[0:TP, slot, k, :].rearrange("p (a e) -> p a e", a=2)
                        w = weight[:, tile, h, k:k + 1]
                        acc = odd[:, :, :] if k % 2 else kv
                        if k < 2:
                            if k == 1:
                                after(steps[0] - 1)
                            step(dve.tensor_scalar(acc, row, w, None, ALU.mult))
                        else:
                            after(steps[0] - 1)
                            step(dve.scalar_tensor_tensor(acc, row, w, acc, ALU.mult, ALU.add))
                    summed[0] += 1
                    if part == 3:
                        signal("rows_used")
                        t.raised("rows_used")
                        step(dve.tensor_tensor(kv, kv, odd[:, :, :], ALU.add))
                        if (h + 1) % H == 0:
                            signal("kv_ready")

            def sum_upto(groups):
                sum_quarters(max(4 * groups - summed[0], 0))

            def ffn_attention(lots):
                for _ in range(2 * PAIRS):
                    t.raised("act_filled")
                dve.wait_ge(act_filled, t.value("act_filled"))
                need("values_moved")
                run_units(False, lots)
                add_projection(h_back)

            def taylor_attention(fill=0):
                layer_norm(h_back, xn)
                t.raised("act_filled")
                sum_quarters(fill)
                for i in range(NT):
                    b = take()
                    step(dve.tensor_copy(QK[:, i, :, :].rearrange("p h d -> p (h d)"), b[0:TP, 0:2 * C]))
                    step(dve.tensor_copy(V1[:, i, :, 1:], b[0:TP, 2 * C:3 * C].rearrange("p (h d) -> p h d", h=H)))
                    drained()
                qk = QK[:, :, :, :].rearrange("p t h d -> p (t h d)")
                step(dve.tensor_tensor(QKsq[:, :, :, :].rearrange("p t h d -> p (t h d)"), qk, qk, ALU.mult))
                after()
                flat = nsq[:, :, :].rearrange("p t h -> p (t h)")
                step(dve.tensor_reduce(flat, QKsq[:, :, :, :].rearrange("p t h d -> p (t h) d"), AX.X, ALU.add))
                after()
                step(dve.tensor_tensor(nsq[:, :, :], nsq[:, :, :],
                                       norm_in[:, :].unsqueeze(1).broadcast_to([TP, NT, 2 * H]), ALU.mult))
                signal("var_ready")
                need("std_ready")
                step(dve.tensor_scalar(nrm[:, :, :], nrm[:, :, :], EPS_NORM, None, ALU.max))
                after()
                step(dve.reciprocal(nrm[:, :, :], nrm[:, :, :]))
                after()
                step(dve.tensor_tensor(nrm[:, :, :], nrm[:, :, :],
                                       norm_out[:, :].unsqueeze(1).broadcast_to([TP, NT, 2 * H]), ALU.mult))
                after()
                flat = QK[:, :, :, :].rearrange("p t h d -> p (t h) d")
                step(dve.tensor_tensor(flat, flat, nrm[:, :, :].rearrange("p t h -> p (t h)").unsqueeze(2)
                                       .broadcast_to([TP, NT * 2 * H, D1]), ALU.mult))
                after()
                for first, phi in ((H, phi_k), (0, phi_q)):
                    step(dve.memset(phi[:, :, :, PHI - 1:], 1.0))
                    for i in range(NT):
                        v = QK[:, i, first:first + H, :]
                        step(dve.tensor_tensor(
                            phi[:, i, :, 0:D1 * D1].rearrange("p h (a b) -> p h a b", a=D1),
                            v.unsqueeze(3).broadcast_to([TP, H, D1, D1]),
                            v.unsqueeze(2).broadcast_to([TP, H, D1, D1]), ALU.mult))
                        step(dve.tensor_copy(phi[:, i, :, D1 * D1:D1 * D1 + D1], v))
                signal("phi_ready")
                sum_quarters(fill)
                b = take()
                step(dve.tensor_scalar(KVM[:, :], b[0:PHI, 0:H * (D1 + 1)], phi_coef[0:PHI, 0:1], None, ALU.mult))
                drained()
                dve.sem_inc(sems["kvm_ready"], 1)
                for _ in range(2 * NT):
                    t.raised("act_filled")
                for i in range(NT):
                    b = take()
                    y = b[0:TP, 0:H * (D1 + 1)].rearrange("p (h d) -> p h d", h=H)
                    step(dve.reciprocal(rden[:, i, :], y[:, :, 0]))
                    after()
                    step(dve.tensor_tensor(Y[:, i, :].rearrange("p (h d) -> p h d", h=H), y[:, :, 1:],
                                           rden[:, i, :].unsqueeze(2).broadcast_to([TP, H, D1]), ALU.mult))
                    drained()
                signal("y_ready")
                sum_quarters(fill)
                t.raised("act_filled")
                b = take()
                step(dve.tensor_tensor(h_back[:, :, :], h_back[:, :, :],
                                       b[0:TP, 0:NT * C].rearrange("p (t c) -> p t c", t=NT), ALU.add))
                drained()

            def experts(fill=0, more=0):
                layer_norm(h_back, xn_moe)
                t.raised("act_filled")
                sum_quarters(fill)
                b = take()
                step(dve.tensor_copy(logits[:, :, :], b[0:TP, 0:NT * NEXP].rearrange("p (t e) -> p t e", t=NT)))
                drained()
                for i in range(NT):
                    step(dve.max(lead[:, i, :], logits[:, i, :]))
                for i in range(NT):
                    after(steps[0] - NT + 1)
                    step(dve.max_index(lead_at[:, i, :], lead[:, i, :], logits[:, i, :]))
                after()
                step(dve.tensor_copy(lead_pos[:, :, :], lead_at[:, :, :]))
                step(dve.tensor_tensor(ldiff[:, :], lead[:, :, 1], lead[:, :, 0], ALU.subtract))
                signal("exp_in")
                need("exp_out")
                step(dve.tensor_scalar(gate1[:, :], lexp[:, :], 1.0, None, ALU.add))
                after()
                step(dve.reciprocal(gate1[:, :], gate1[:, :]))
                after()
                step(dve.tensor_tensor(gate2[:, :], lexp[:, :], gate1[:, :], ALU.mult))
                after()
                for i in range(NT):
                    for k, w, dst in ((0, gate1, gates), (1, gate2, gates2)):
                        step(dve.tensor_scalar(dst[:, i, :], iota[:, 0:NEXP], lead_pos[:, i, k:k + 1], w[:, i:i + 1],
                                               ALU.is_equal, ALU.mult))
                after()
                step(dve.tensor_tensor(gates[:, :, :], gates[:, :, :], gates2[:, :, :], ALU.add))
                signal("gates_ready")
                sum_quarters(more)
                for _ in range(NEXP + 1):
                    t.raised("act_filled")
                for i in range(NT):
                    for half in range(2):
                        b = take()
                        step(dve.tensor_tensor(
                            weighed[:, half * 8:half * 8 + 8, :], b[0:TP, :].rearrange("p (e c) -> p e c", e=8),
                            gates[:, i, half * 8:half * 8 + 8].unsqueeze(2).broadcast_to([TP, 8, C]), ALU.mult))
                        drained()
                    step(dve.tensor_reduce(moe[:, i, :], weighed[:, :, :].rearrange("p e c -> p c e"), AX.X, ALU.add))
                    after()
                b = take()
                step(dve.tensor_tensor(moe[:, :, :], moe[:, :, :],
                                       b[0:TP, 0:NT * C].rearrange("p (t c) -> p t c", t=NT), ALU.add))
                drained()
                step(dve.tensor_tensor(moe[:, :, :], moe[:, :, :], xn_moe[:, :, :], ALU.add))
                after()
                layer_stats(moe)
                for i in range(NT):
                    step(dve.tensor_scalar(moe[:, i, :], moe[:, i, :], bagg[:, i, 0:1], rstd[:, i:i + 1],
                                           ALU.subtract, ALU.mult))
                after()
                step(dve.tensor_tensor(moe[:, :, :], moe[:, :, :],
                                       Gamma1[:, :].unsqueeze(1).broadcast_to([TP, NT, C]), ALU.mult))
                after()
                step(dve.tensor_tensor(moe[:, :, :], moe[:, :, :],
                                       Beta1[:, :].unsqueeze(1).broadcast_to([TP, NT, C]), ALU.add))
                after()
                stored = t.n.get("out_ready", 0)
                dve.wait_ge(out_stored, (t.value("out_ready", stored) + 1) * 16)
                step(dve.tensor_tensor(outb[:, :, :], h_back[:, :, :], moe[:, :, :], ALU.add))
                signal("out_ready")
                t.raised("out_ready")

            def move(dst, src):
                step(dve.tensor_copy(dst[:, :, :], src[:, :, :]))
                after()

            def start():
                dve.wait_ge(weights_loaded, 16 * N_LOADS)
                dve.wait_ge(consts_made, N_CONST)
                made = [0]

                def make(ins):
                    ins.then_inc(dve_consts, 1)
                    made[0] += 1

                for i in (0, 3, 4):
                    make(dve.memset(xT[i][C:C + 1, :], 1.0))
                make(dve.memset(mean_of_c[:, :], 1.0 / C))
                make(dve.memset(eps_conv[:, :], EPS_CONV))
                make(dve.memset(eps_ln[:, :], EPS_LN))
                make(dve.memset(norm_in[:, 0:H], float(D1) ** 0.5))
                make(dve.memset(norm_in[:, H:], 1.0))
                make(dve.tensor_scalar(norm_out[:, 0:H], norm_out[:, 0:H], float(D1) ** 0.5, None, ALU.mult))
                make(dve.memset(norm_out[:, H:], float(D1) ** 0.25))
                make(dve.memset(V1[:, :, :, 0:1], 1.0))
                make(dve.memset(odd[:, :, :], 0.0))
                assert made[0] == N_DVE_CONST, made
                dve.wait_ge(dve_consts, N_DVE_CONST)
                dve.sem_inc(out_stored, 16)
                conv_stage()
                attention0(lambda u: 0)
                key_norm()
                keys_filled[0] = t.n["act_filled"]
                for tile in range(NT):
                    keys(tile)
                end()

            def iteration(front, back):
                begin()
                act_base[0] = t.n["act_filled"]
                summed[0] = 0
                if back:
                    move(h_back, h_mid)
                move(h_mid, h_front)
                if back:
                    ffn_attention(lambda u: 1)
                if front:
                    conv_stage()
                    attention0(lambda u: min(u % 3, 1), 6)
                sum_upto(H)
                if front:
                    key_norm()
                    keys_filled[0] = t.n["act_filled"]
                    keys(0)
                if back:
                    taylor_attention(4)
                    experts(5, 15)
                sum_upto(2 * H)
                if front:
                    keys(1)
                sum_upto(3 * H)
                if front:
                    keys(2)
                end()

            def finish():
                begin()
                act_base[0] = t.n["act_filled"]
                move(h_back, h_mid)
                ffn_attention(lambda u: 0)
                taylor_attention()
                experts()

            run(t, dve, start, iteration, finish)


def kernel(**inputs):
    import numpy as _np
    import concourse.bacc as _bacc
    from concourse import mybir as _mybir
    from concourse.bass_utils import run_bass_kernel_spmd as _run

    g = {k: _np.asarray(v) for k, v in inputs.items()}
    row = lambda a: a.reshape(1, -1)
    col = lambda a: a.reshape(-1, 1)
    arrays = {
        "x": g["x"].transpose(0, 2, 1),
        "conv_w": g["L0_tok_w"][:, 0, :].T,
        "conv_b": col(g["L0_tok_b"]), "gamma0": col(g["L0_tok_gamma"]), "beta0": col(g["L0_tok_beta"]),
        "alpha0": col(g["L0_tok_alpha"]),
        "wq": g["L0_attn_Wq"], "bq": row(g["L0_attn_bq"]), "wk": g["L0_attn_Wk"], "bk": row(g["L0_attn_bk"]),
        "wv": g["L0_attn_Wv"], "bv": row(g["L0_attn_bv"]), "wu": g["L0_attn_Wu"], "bu": row(g["L0_attn_bu"]),
        "wpk_t": g["L0_ffn_Wq_pk"].reshape(64, 16, 32).transpose(2, 1, 0),
        "pk_keys_t": g["L0_ffn_pk_keys"].transpose(3, 0, 2, 1).reshape(32, 16, 64),
        "wq2": g["L0_ffn_Wq"],
        "kv_table": _np.concatenate([g["L0_ffn_keys_table"], g["L0_ffn_values_table"]], axis=1),
        "wo": g["L0_ffn_Wo"],
        "wqkv_t": g["L1_attn_Wqkv"].T, "bqkv": row(g["L1_attn_bqkv"]),
        "wproj_t": g["L1_attn_Wproj"].T, "bproj": row(g["L1_attn_bproj"]),
        "temperature": row(g["L1_attn_temperature"]),
        "gate_w": g["L1_ffn_gate_w"], "gate_b": row(g["L1_ffn_gate_b"]),
        "w1": g["L1_ffn_w1"], "b1": g["L1_ffn_b1"], "w2": g["L1_ffn_w2"], "b2": g["L1_ffn_b2"],
        "gamma1": row(g["L1_ffn_gamma"]), "beta1": row(g["L1_ffn_beta"]),
    }
    nc = _bacc.Bacc("TRN2", target_bir_lowering=False, num_devices=1)
    args, feeds = [], {}
    for name, a in arrays.items():
        a = _np.ascontiguousarray(a)
        feeds[f"in_{name}"] = a
        args.append(nc.dram_tensor(f"in_{name}", a.shape, _mybir.dt.from_np(a.dtype), kind="ExternalInput").ap())
    o = nc.dram_tensor("out_0", (BATCH, T, C), F32, kind="ExternalOutput").ap()
    build(nc, *args, o)
    r = _run(nc, [feeds], core_ids=[0])
    return r.results[0]["out_0"]
```

```python
from contextlib import ExitStack

import concourse.bass as bass
from concourse import mybir

F32 = mybir.dt.float32
BF16 = mybir.dt.bfloat16
F16 = mybir.dt.float16
U32 = mybir.dt.uint32
ALU = mybir.AluOpType
ACT = mybir.ActivationFunctionType
AX = mybir.AxisListType

BATCH, T_IN, T, C = 16, 750, 375, 64
TAPS = 5
TP = 125
NT = T // TP
H, E = 8, 64
HE = H * E
PAIRS = H // 2
DK, NKEYS, TOPK = 32, 64, 16
GROUPS = 2 * H
CAND = [TOPK // (i + 1) for i in range(TOPK)]
NCAND = sum(CAND)
D1 = 8
PHI = D1 * D1 + D1 + 1
NEXP, F = 16, 128
RING = 6
BANKS = 4
MASKED = -1e30
KEY_BIAS = NKEYS * NKEYS // 2
EPS_CONV, EPS_LN, EPS_NORM = 1e-3, 1e-5, 1e-12
PER = {"act_filled": 155, "dve_filled": 30, "max_ready": 48, "kv_ready": 3, "indices_ready": 3,
       "xn_ready": 4, "var_ready": 7, "std_ready": 7, "o_ready": 6, "taps_done": 1, "conv_ready": 2,
       "exp_in": 4, "exp_out": 4, "phi_ready": 1, "gates_ready": 1, "y_ready": 1, "rows_used": 24,
       "kvm_ready": 1, "out_ready": 1, "x_loaded": 1, "values_moved": 1}


class Tally:

    def __init__(self):
        self.n, self.turn = {}, None

    def raised(self, name):
        self.n[name] = self.n.get(name, 0) + 1

    def value(self, name, k=None):
        k = self.n.get(name, 0) if k is None else k
        return k if self.turn is None else self.turn * PER[name] + k

    def loop(self, turn):
        self.turn, self.before = turn, dict(self.n)

    def end(self, turns):
        for name in self.n:
            per = self.n[name] - self.before.get(name, 0)
            assert per == PER[name], (name, per)
            self.n[name] += (turns - 1) * per
        self.turn = None


def build(nc, x, conv_w, conv_b, gamma0, beta0, alpha0, wq, bq, wk, bk, wv, bv, wu, bu,
          wpk_t, pk_keys_t, wq2, kv_table, wo, wqkv_t, bqkv, wproj_t, bproj, temperature,
          gate_w, gate_b, w1, b1, w2, b2, gamma1, beta1, out):
    with ExitStack() as ctx:
        def sb(name, shape, dtype=F32):
            return ctx.enter_context(nc.sbuf_tensor(name, shape, dtype))

        def sem(name):
            return ctx.enter_context(nc.semaphore(name))

        ident = sb("ident", [128, 128])
        identb = sb("identb", [128, 128], BF16)
        mask_strict = sb("mask_strict", [TP, TP], BF16)
        mask_causal = sb("mask_causal", [TP, TP], BF16)
        row_live = sb("row_live", [TP, 1])
        mean_of_c = sb("mean_of_c", [C, C])
        eps_conv = sb("eps_conv", [C, 1])
        eps_ln = sb("eps_ln", [TP, 1])
        iota = sb("iota", [TP, NEXP])
        iota_cand = sb("iota_cand", [TP, NCAND, H], F16)
        head_offset = sb("head_offset", [TP, H * TOPK])
        norm_in = sb("norm_in", [TP, 2 * H])
        norm_out = sb("norm_out", [TP, 2 * H])
        phi_coef = sb("phi_coef", [PHI, 1])
        taps_w = sb("taps_w", [C, TAPS])
        chan = sb("chan", [C, 4])
        Wq = sb("Wq", [C + 1, HE])
        Wk = sb("Wk", [C + 1, HE])
        Wv = sb("Wv", [C + 1, HE])
        Wu = sb("Wu", [128, PAIRS, C])
        Bu = sb("Bu", [C + 1, C])
        Wpk = sb("Wpk", [C, GROUPS * NKEYS])
        Wq2 = sb("Wq2", [C, HE])
        Wo = sb("Wo", [128, PAIRS, C])
        Wqkv = sb("Wqkv", [C + 1, 3 * C])
        Wproj = sb("Wproj", [C + 1, C])
        Wgate = sb("Wgate", [C + 1, NEXP])
        W1 = sb("W1", [C + 1, NEXP, F])
        W2 = sb("W2", [F, NEXP, C])
        B2 = sb("B2", [NEXP, C])
        Gamma1 = sb("Gamma1", [TP, C])
        Beta1 = sb("Beta1", [TP, C])

        xpad = sb("xpad", [C, T_IN + 4])
        conv = sb("conv", [C, T])
        conv_neg = sb("conv_neg", [C, T])
        cstat = sb("cstat", [C, 6])
        cmom = sb("cmom", [C, 2])
        call = sb("call", [C, 8])
        h_front = sb("h_front", [TP, NT, C])
        h_mid = sb("h_mid", [TP, NT, C])
        h_back = sb("h_back", [TP, NT, C])
        bstat = sb("bstat", [TP, NT, 6])
        bagg = sb("bagg", [TP, NT, 2])
        std = sb("std", [TP, NT])
        rstd = sb("rstd", [TP, NT])
        xn = sb("xn", [TP, NT, C])
        xn_moe = sb("xn_moe", [TP, NT, C])
        xT = [sb(f"xT{i}", [C + 1, T]) for i in range(5)]
        QKT = sb("QKT", [128, 2, PAIRS, T])
        QT, KT = QKT[:, 0, :, :], QKT[:, 1, :, :]
        Vbuf = sb("Vbuf", [TP, NT * H * PHI])
        V = Vbuf[:, 0:NT * HE].rearrange("p (t n) -> p t n", t=NT)
        negmax = sb("negmax", [TP, 4])
        sums = sb("sums", [TP, NT, H])
        rsum = sb("rsum", [TP, NT, H])
        probs = sb("probs", [TP, 2, T])
        probsT = sb("probsT", [TP, 2, T])
        O = sb("O", [TP, NT, HE])
        OTbuf = sb("OTbuf", [128, NT * H * PHI])
        OT = OTbuf[:, 0:NT * PAIRS * TP].rearrange("p (t n) -> p t n", t=NT)
        wide = sb("wide", [128, NEXP * T])
        scores = sb("scores", [TP, NT, GROUPS * NKEYS])
        top = sb("top", [TP, GROUPS, TOPK])
        top_at = sb("top_at", [TP, GROUPS, TOPK], U32)
        top_key = sb("top_key", [TP, GROUPS, TOPK])
        cand = sb("cand", [TP, H, NCAND])
        cand_key = sb("cand_key", [TP, NCAND, H], F16)
        best = sb("best", [TP, H, TOPK])
        best_at = sb("best_at", [TP, H, TOPK], U32)
        best_pos = sb("best_pos", [TP, TOPK, H], F16)
        onehot = wide[0:TP, 0:H * TOPK * NCAND // 2].bitcast(F16).rearrange("p (c k h) -> p c k h", c=NCAND, k=TOPK)
        below = sb("below", [TP, H, TOPK])
        expd = sb("expd", [TP, H, TOPK])
        esum = sb("esum", [TP, H])
        weight = sb("weight", [TP, NT, H, TOPK])
        index = sb("index", [128, NT, H * TOPK], U32)
        rows = sb("rows", [128, RING, TOPK, 2 * E])
        Wpk_t = rows[0:DK, 0, 0:8, :].rearrange("p k (n c) -> p (k n) c", c=C)
        Keys_t = rows[0:DK, 0, 8:16, :].rearrange("p k (n c) -> p (k n) c", c=NKEYS)
        KV = sb("KV", [TP, NT, 2, HE])
        odd = sb("odd", [TP, 2, E])
        QK = sb("QK", [TP, NT, 2 * H, D1])
        QKsq = sb("QKsq", [TP, NT, 2 * H, D1])
        V1 = sb("V1", [TP, NT, H, D1 + 1])
        nsq = sb("nsq", [TP, NT, 2 * H])
        nrm = sb("nrm", [TP, NT, 2 * H])
        phi_k = Vbuf[:, :].rearrange("p (t h f) -> p t h f", t=NT, h=H)
        phi_q = OTbuf[0:TP, :].rearrange("p (t h f) -> p t h f", t=NT, h=H)
        phi_qT = QKT[0:PHI, :, :, :].rearrange("p a g n -> p (a g n)").rearrange("p (t n) -> p t n", t=NT)
        KVM = sb("KVM", [PHI, H * (D1 + 1)])
        rden = sb("rden", [TP, NT, H])
        Y = sb("Y", [TP, NT, C])
        logits = sb("logits", [TP, NT, NEXP])
        lead = sb("lead", [TP, NT, 8])
        lead_at = sb("lead_at", [TP, NT, 8], U32)
        lead_pos = sb("lead_pos", [TP, NT, 8])
        ldiff = sb("ldiff", [TP, NT])
        lexp = sb("lexp", [TP, NT])
        gate1 = sb("gate1", [TP, NT])
        gate2 = sb("gate2", [TP, NT])
        gates = sb("gates", [TP, NT, NEXP])
        gates2 = sb("gates2", [TP, NT, NEXP])
        gatesT = sb("gatesT", [NEXP, T])
        hidden = wide[:, 0:NEXP * T].rearrange("p (e n) -> p e n", e=NEXP)
        weighed = O[:, 0:2, :].rearrange("p t (e c) -> p (t e) c", c=C)
        moe = sb("moe", [TP, NT, C])
        outb = sb("outb", [TP, NT, C])

        act_bank = [ctx.enter_context(nc.psum_tensor(f"act_bank{i}", [128, 512], F32)) for i in range(BANKS)]
        dve_bank = [ctx.enter_context(nc.psum_tensor(f"dve_bank{i}", [128, 512], F32)) for i in range(BANKS)]

        weights_loaded = sem("weights_loaded")
        late_loaded = sem("late_loaded")
        consts_made = sem("consts_made")
        keys_folded = sem("keys_folded")
        dve_consts = sem("dve_consts")
        x_loaded = sem("x_loaded")
        out_stored = sem("out_stored")
        act_filled = sem("act_filled")
        act_drained = sem("act_drained")
        dve_filled = sem("dve_filled")
        dve_drained = sem("dve_drained")
        pool_passed = sem("pool_passed")
        pe_passed = sem("pe_passed")
        dve_step = sem("dve_step")
        sems = {n: sem(n) for n in PER if n not in ("act_filled", "dve_filled", "x_loaded")}
        sems.update(act_filled=act_filled, dve_filled=dve_filled)
        landed = [sem(f"rows_landed{i}") for i in range(RING)]

        block = ctx.enter_context(nc.Block())
        N_CONST, N_DVE_CONST = 18, 11

        def run(t, eng, start, iteration, finish):
            start()
            iteration(True, False)
            with eng.Fori(0, BATCH - 2) as turn:
                t.loop(turn)
                iteration(True, True)
                t.end(BATCH - 2)
            iteration(False, True)
            finish()

        ALL = (0, 1, 2)

        def columns(tiles):
            return slice(tiles[0] * TP, (tiles[-1] + 1) * TP)

        loads = [(taps_w[:, :], conv_w), (chan[:, 0:1], conv_b), (chan[:, 1:2], gamma0),
                 (chan[:, 2:3], beta0), (chan[:, 3:4], alpha0),
                 (Wq[0:C, :], wq), (Wq[C:C + 1, :], bq), (Wk[0:C, :], wk), (Wk[C:C + 1, :], bk),
                 (Wv[0:C, :], wv), (Wv[C:C + 1, :], bv), (Bu[C:C + 1, :], bu),
                 (Wu[:, :, :], wu.rearrange("(g p) c -> p g c", p=128)),
                 (Wpk_t[:, :, :], wpk_t), (Keys_t[:, :, :], pk_keys_t)]
        late_loads = [
                 (Wq2[:, :], wq2),
                 (Wo[:, :, :], wo.rearrange("(g p) c -> p g c", p=128)),
                 (Wqkv[0:C, :], wqkv_t), (Wqkv[C:C + 1, :], bqkv),
                 (Wproj[0:C, :], wproj_t), (Wproj[C:C + 1, :], bproj),
                 (norm_out[:, 0:H], temperature.broadcast_to([TP, H])),
                 (Wgate[0:C, :], gate_w), (Wgate[C:C + 1, :], gate_b),
                 (W1[0:C, :, :], w1.rearrange("e c f -> c e f")),
                 (W1[C:C + 1, :, :], b1.rearrange("(o e) f -> o e f", o=1)),
                 (W2[:, :, :], w2.rearrange("e f c -> f e c")), (B2[:, :], b2),
                 (Gamma1[:, :], gamma1.broadcast_to([TP, C])), (Beta1[:, :], beta1.broadcast_to([TP, C]))]
        n_loads, n_late = len(loads), len(late_loads)

        @block.sync
        def _(sp):
            sp.wait_ge(consts_made, N_CONST)
            sp.dma_start(xpad[:, 1:1 + T_IN], x[0]).then_inc(x_loaded, 16)
            for dst, src in loads[0::2]:
                sp.dma_start(dst, src).then_inc(weights_loaded, 16)
            for dst, src in late_loads[0::2]:
                sp.dma_start(dst, src).then_inc(late_loaded, 16)

            def load(b, n):
                sp.wait_ge(sems["taps_done"], n)
                sp.dma_start(xpad[:, 1:1 + T_IN], x[b]).then_inc(x_loaded, 16)

            def store(b, n):
                sp.wait_ge(sems["out_ready"], n)
                sp.dma_start(out[b].rearrange("(t p) c -> p t c", p=TP), outb[:, :, :]).then_inc(out_stored, 16)

            for b in (1, 2):
                load(b, b)
            with sp.Fori(0, BATCH - 3) as i:
                load(i + 3, i + 3)
                store(i, i + 1)
            for b in range(BATCH - 3, BATCH):
                store(b, b + 1)
            sp.wait_ge(out_stored, 16 * (BATCH + 1))

        @block.gpsimd
        def _(pool):
            done = [0]

            def made(ins):
                ins.then_inc(consts_made, 1)
                done[0] += 1

            for m in (ident, identb):
                made(pool.memset(m[:, :], 1.0))
            for m in (mask_strict, mask_causal):
                made(pool.memset(m[:, :], 0.0))
            made(pool.memset(row_live[:, :], 1.0))
            made(pool.iota(iota[:, :], [[1, NEXP]], base=0, channel_multiplier=0,
                           allow_small_or_imprecise_dtypes=True))
            made(pool.iota(iota_cand[:, :, :], [[1, NCAND], [0, H]], base=0, channel_multiplier=0,
                           allow_small_or_imprecise_dtypes=True))
            made(pool.iota(head_offset[:, :].rearrange("p (h k) -> p h k", h=H), [[NKEYS * NKEYS, H], [0, TOPK]],
                           base=KEY_BIAS, channel_multiplier=0, allow_small_or_imprecise_dtypes=True))
            made(pool.memset(index[:, :, :], 0))
            made(pool.memset(xpad[:, :], 0.0))
            made(pool.memset(phi_coef[:, :], D1 / T))
            pool.wait_ge(consts_made, done[0])
            for m in (ident, identb):
                made(pool.affine_select(out=m[:, :], in_=m[:, :], compare_op=ALU.is_equal, fill=0.0,
                                        base=0, pattern=[[-1, 128]], channel_multiplier=1))
            for m, first in ((mask_strict, -1), (mask_causal, 0)):
                made(pool.affine_select(out=m[:, :], in_=m[:, :], compare_op=ALU.is_ge, fill=MASKED,
                                        base=first, pattern=[[-1, TP]], channel_multiplier=1))
            made(pool.affine_select(out=row_live[:, :], in_=row_live[:, :], compare_op=ALU.is_gt, fill=0.0,
                                    base=0, pattern=[[0, 1]], channel_multiplier=1))
            made(pool.affine_select(out=phi_coef[:, :], in_=phi_coef[:, :], compare_op=ALU.is_ge,
                                    fill=float(D1) ** 0.5 / T, base=-(D1 * D1 + D1), pattern=[[0, 1]],
                                    channel_multiplier=1))
            pool.wait_ge(consts_made, done[0])
            made(pool.affine_select(out=phi_coef[:, :], in_=phi_coef[:, :], compare_op=ALU.is_ge,
                                    fill=0.5 / T, base=-D1 * D1, pattern=[[0, 1]], channel_multiplier=1))
            assert done[0] == N_CONST, done

            t = Tally()
            def gather(front, back):
                for tile in range(NT):
                    t.raised("indices_ready")
                    for h in range(H):
                        slot = (tile * H + h) % RING
                        if h == 0:
                            pool.wait_ge(sems["indices_ready"], t.value("indices_ready"))
                            pool.sem_inc(pool_passed, 1)
                        used = t.n.get("rows_used", 0) - RING + 1
                        if used > 0:
                            pool.wait_ge(sems["rows_used"], t.value("rows_used", used))
                            pool.sem_inc(pool_passed, 1)
                        t.raised("rows_used")
                        for k in range(TOPK):
                            at = h * TOPK + k
                            pool.indirect_dma_start(
                                rows[:, slot, k, :], None, kv_table,
                                bass.IndirectOffsetOnAxis(index[:, tile, at:at + 1], 0)).then_inc(landed[slot], 16)

            run(t, pool, lambda: None, gather, lambda: None)

        @block.tensor
        def _(pe):
            t = Tally()
            turn_base = {"act": 0, "dve": 0}

            def begin():
                turn_base["act"], turn_base["dve"] = t.n.get("act_filled", 0), t.n.get("dve_filled", 0)

            def bank(which):
                name = which + "_filled"
                n, base = t.n.get(name, 0), turn_base[which]
                free = max(n - BANKS + 1, base)
                if free > 0:
                    pe.wait_ge(act_drained if which == "act" else dve_drained, t.value(name, free))
                    pe.sem_inc(pe_passed, 1)
                return (act_bank if which == "act" else dve_bank)[(n - base) % BANKS]

            def full(which, ins):
                ins.then_inc(sems[which + "_filled"], 1)
                t.raised(which + "_filled")

            def drained(which, k=None):
                pe.wait_ge(act_drained if which == "act" else dve_drained, t.value(which + "_filled", k))
                pe.sem_inc(pe_passed, 1)

            def need(name):
                t.raised(name)
                pe.wait_ge(sems[name], t.value(name))
                pe.sem_inc(pe_passed, 1)

            def turn_tiles(src, tiles=ALL):
                b = bank("act")
                for i in tiles:
                    ins = pe.transpose(b[0:C, i * TP:(i + 1) * TP], src[:, i, :], ident[0:TP, 0:TP])
                full("act", ins)

            def units(mask, tiles=ALL):
                n_units, out_bank = len(tiles) * H, None
                for u in range(n_units + 2):
                    if u < n_units:
                        tile, h = tiles[u // H], u % H
                        g, p = h // 2, 64 * (h % 2)
                        b = bank("act")
                        n = (tile + 1) * TP
                        pe.matmul(b[0:TP, 0:n], QT[p:p + E, g, tile * TP:n], KT[p:p + E, g, 0:n],
                                  start=True, stop=False)
                        full("act", pe.matmul(b[0:TP, n - TP:n], identb[0:TP, 0:TP], mask[:, :],
                                              start=False, stop=True))
                    if 1 <= u <= n_units:
                        tile, h = tiles[(u - 1) // H], (u - 1) % H
                        b = bank("act")
                        drained("act", t.n["act_filled"] - (2 if 1 < u < n_units else 1))
                        for j in range(tile + 1):
                            ins = pe.transpose(b[0:TP, j * TP:(j + 1) * TP],
                                               probs[:, (u - 1) % 2, j * TP:(j + 1) * TP], ident[0:TP, 0:TP])
                        full("act", ins)
                    if u >= 2:
                        tile, h = tiles[(u - 2) // H], (u - 2) % H
                        if h == 0:
                            out_bank = bank("dve")
                        drained("act", t.n["act_filled"] - (2 if u < n_units else 1 if u == n_units else 0))
                        for j in range(tile + 1):
                            ins = pe.matmul(out_bank[0:TP, h * E:(h + 1) * E],
                                            probsT[:, (u - 2) % 2, j * TP:(j + 1) * TP], V[:, j, h * E:(h + 1) * E],
                                            start=(j == 0), stop=(j == tile))
                        if h == H - 1:
                            full("dve", ins)

            def project(w, bias, tiles=ALL):
                for tile in tiles:
                    need("o_ready")
                    b = bank("act")
                    for g in range(PAIRS):
                        ins = pe.transpose(b[:, g * TP:(g + 1) * TP], O[:, tile, g * 128:(g + 1) * 128],
                                           ident[0:TP, 0:TP])
                    full("act", ins)
                drained("act")
                for tile in tiles:
                    b = bank("dve")
                    for g in range(PAIRS):
                        ins = pe.matmul(b[0:TP, 0:C], OT[:, tile, g * TP:(g + 1) * TP], w[:, g, :],
                                        start=(g == 0), stop=(g == PAIRS - 1 and not bias))
                    if bias:
                        ins = pe.matmul(b[0:TP, 0:C], xT[0][C:C + 1, tile * TP:(tile + 1) * TP],
                                        Bu[C:C + 1, :], start=False, stop=True)
                    full("dve", ins)

            def transposed_heads(w, k, src):
                for g in range(PAIRS):
                    full("act", pe.matmul(bank("act")[:, 0:T], w[0:k, g * 128:(g + 1) * 128], src[0:k, :],
                                          start=True, stop=True))

            def attention0(first=ALL):
                need("xn_ready")
                turn_tiles(xn)
                drained("act")
                transposed_heads(Wq, C + 1, xT[0])
                transposed_heads(Wk, C + 1, xT[0])
                for tile in range(NT):
                    full("act", pe.matmul(bank("act")[0:TP, :], xT[0][:, tile * TP:(tile + 1) * TP], Wv[:, :],
                                          start=True, stop=True))
                drained("act")
                units(mask_strict, first)
                project(Wu, True, first)

            def conv_stage():
                need("conv_ready")
                full("dve", pe.matmul(bank("dve")[0:C, 0:2], mean_of_c[:, :], cmom[:, :], start=True, stop=True))
                need("conv_ready")
                b = bank("dve")
                for i in range(NT):
                    ins = pe.transpose(b[0:TP, i * C:(i + 1) * C], conv[:, i * TP:(i + 1) * TP], ident[0:C, 0:C])
                full("dve", ins)

            def key_scores(tiles=ALL):
                need("xn_ready")
                turn_tiles(xn, tiles)
                drained("act")
                for tile in tiles:
                    for half in range(2):
                        full("act", pe.matmul(bank("act")[0:TP, :], xT[1][0:C, tile * TP:(tile + 1) * TP],
                                              Wpk[:, half * 512:(half + 1) * 512], start=True, stop=True))

            def ffn_attention(tiles=ALL):
                if 0 in tiles:
                    transposed_heads(Wq2, C, xT[2])
                for g in range(PAIRS):
                    b = bank("act")
                    for i in tiles:
                        ins = pe.transpose(b[:, i * TP:(i + 1) * TP], KV[:, i, 0, g * 128:(g + 1) * 128],
                                           ident[0:TP, 0:TP])
                    full("act", ins)
                drained("act")
                need("values_moved")
                units(mask_causal, tiles)
                project(Wo, False, tiles)

            def taylor_attention():
                need("xn_ready")
                turn_tiles(xn)
                drained("act")
                for i in range(NT):
                    full("dve", pe.matmul(bank("dve")[0:TP, 0:3 * C], xT[3][:, i * TP:(i + 1) * TP], Wqkv[:, :],
                                          start=True, stop=True))
                need("phi_ready")
                b = bank("dve")
                for h in range(H):
                    for i in range(NT):
                        ins = pe.matmul(b[0:PHI, h * 9:h * 9 + 9], phi_k[:, i, h, :], V1[:, i, h, :],
                                        start=(i == 0), stop=(i == NT - 1))
                full("dve", ins)
                for i in range(NT):
                    for half in range(2):
                        b = bank("act")
                        for j in range(4):
                            ins = pe.transpose(b[0:PHI, j * TP:(j + 1) * TP], phi_q[:, i, half * 4 + j, :],
                                               ident[0:TP, 0:TP])
                        full("act", ins)
                drained("act")
                need("kvm_ready")
                for i in range(NT):
                    b = bank("dve")
                    for h in range(H):
                        ins = pe.matmul(b[0:TP, h * 9:h * 9 + 9], phi_qT[:, i, h * TP:(h + 1) * TP],
                                        KVM[:, h * 9:h * 9 + 9], start=True, stop=True)
                    full("dve", ins)
                need("y_ready")
                turn_tiles(Y)
                drained("act")
                b = bank("dve")
                for i in range(NT):
                    ins = pe.matmul(b[0:TP, i * C:(i + 1) * C], xT[4][:, i * TP:(i + 1) * TP], Wproj[:, :],
                                    start=True, stop=True)
                full("dve", ins)

            def experts():
                need("xn_ready")
                turn_tiles(xn_moe)
                drained("act")
                b = bank("dve")
                for i in range(NT):
                    ins = pe.matmul(b[0:TP, i * NEXP:(i + 1) * NEXP], xT[3][:, i * TP:(i + 1) * TP],
                                    Wgate[:, :], start=True, stop=True)
                full("dve", ins)
                for e in range(NEXP):
                    full("act", pe.matmul(bank("act")[:, 0:T], W1[:, e, :], xT[3][:, :], start=True, stop=True))
                need("gates_ready")
                b = bank("act")
                for i in range(NT):
                    ins = pe.transpose(b[0:NEXP, i * TP:(i + 1) * TP], gates[:, i, :], ident[0:TP, 0:TP])
                full("act", ins)
                drained("act")
                for i in range(NT):
                    for half in range(2):
                        b = bank("dve")
                        for j in range(8):
                            e = half * 8 + j
                            ins = pe.matmul(b[0:TP, j * C:(j + 1) * C], hidden[:, e, i * TP:(i + 1) * TP],
                                            W2[:, e, :], start=True, stop=True)
                        full("dve", ins)
                b = bank("dve")
                for i in range(NT):
                    ins = pe.matmul(b[0:TP, i * C:(i + 1) * C], gatesT[:, i * TP:(i + 1) * TP], B2[:, :],
                                    start=True, stop=True)
                full("dve", ins)

            def start():
                pe.wait_ge(weights_loaded, 16 * n_loads)
                pe.wait_ge(consts_made, N_CONST)
                for g in range(GROUPS):
                    bk = act_bank[g // 8]
                    ins = pe.matmul(bk[0:C, (g % 8) * NKEYS:(g % 8 + 1) * NKEYS], Wpk_t[:, g, :], Keys_t[:, g, :],
                                    start=True, stop=True)
                ins.then_inc(keys_folded, 1)
                pe.wait_ge(keys_folded, 3)
                pe.wait_ge(dve_consts, N_DVE_CONST)
                conv_stage()
                attention0((0,))
                key_scores((0,))
                units(mask_strict, (1, 2))
                project(Wu, True, (1, 2))
                key_scores((1, 2))
                pe.wait_ge(late_loaded, 16 * n_late)

            def iteration(front, back):
                begin()
                if back:
                    for i in range(NT):
                        need("kv_ready")
                    ffn_attention()
                if front:
                    conv_stage()
                    attention0()
                    key_scores()
                if back:
                    taylor_attention()
                    experts()

            def finish():
                begin()
                for i in range(NT - 1):
                    need("kv_ready")
                ffn_attention((0, 1))
                need("kv_ready")
                ffn_attention((2,))
                taylor_attention()
                experts()

            run(t, pe, start, iteration, finish)

        @block.scalar
        def _(act):
            t = Tally()
            base = [0]
            for dst, src in loads[1::2]:
                act.dma_start(dst, src).then_inc(weights_loaded, 16)
            for dst, src in late_loads[1::2]:
                act.dma_start(dst, src).then_inc(late_loaded, 16)
            act.wait_ge(weights_loaded, 16 * n_loads)
            act.wait_ge(consts_made, N_CONST)

            def begin():
                base[0] = t.n.get("act_filled", 0)

            def take():
                k = t.n.get("act_filled", 0)
                t.raised("act_filled")
                act.wait_ge(act_filled, t.value("act_filled"))
                return act_bank[(k - base[0]) % BANKS]

            def copy_out(dst, src, func=ACT.Copy, scale=1.0):
                act.activation(dst, src, func, scale=scale).then_inc(act_drained, 1)

            def need(name):
                t.raised(name)
                act.wait_ge(sems[name], t.value(name))

            def std_of(dst, src, eps):
                need("var_ready")
                act.activation(dst, src, ACT.Sqrt, bias=eps).then_inc(sems["std_ready"], 1)

            def layer_norm(tiles=ALL):
                lo, hi = tiles[0], tiles[-1] + 1
                std_of(std[:, lo:hi], bagg[:, lo:hi, 1], eps_ln[:, 0:1])

            def exp_of(dst, src):
                need("exp_in")
                act.activation(dst, src, ACT.Exp).then_inc(sems["exp_out"], 1)

            def units(tiles=ALL):
                for u in range(len(tiles) * H + 1):
                    if u < len(tiles) * H:
                        tile, h = tiles[u // H], u % H
                        n = (tile + 1) * TP
                        b = take()
                        need("max_ready")
                        act.activation(probs[:, u % 2, 0:n], b[0:TP, 0:n], ACT.Exp, bias=negmax[:, u % 4:u % 4 + 1],
                                       accum_out=sums[:, tile, h:h + 1]).then_inc(act_drained, 1)
                    if u >= 1:
                        n = (tiles[(u - 1) // H] + 1) * TP
                        copy_out(probsT[:, (u - 1) % 2, 0:n], take()[0:TP, 0:n])

            def project(tiles=ALL):
                for tile in tiles:
                    copy_out(OT[:, tile, :], take()[:, 0:PAIRS * TP])

            def attention0(first=ALL):
                layer_norm()
                copy_out(xT[0][0:C, :], take()[0:C, 0:T])
                for g in range(PAIRS):
                    copy_out(QT[:, g, :], take()[:, 0:T], scale=float(E) ** -0.5)
                for g in range(PAIRS):
                    copy_out(KT[:, g, :], take()[:, 0:T])
                for tile in range(NT):
                    copy_out(V[:, tile, :], take()[0:TP, :])
                units(first)
                project(first)

            def conv_stage():
                std_of(call[:, 3:4], call[:, 2:3], eps_conv[:, 0:1])

            def key_scores(tiles=ALL):
                layer_norm(tiles)
                copy_out(xT[1][0:C, columns(tiles)], take()[0:C, columns(tiles)])
                for tile in tiles:
                    for half in range(2):
                        copy_out(scores[:, tile, half * 512:(half + 1) * 512], take()[0:TP, :])

            def key_exp():
                exp_of(expd[:, :, :], below[:, :, :])

            def ffn_attention(tiles=ALL):
                for i in tiles:
                    need("kv_ready")
                lo, hi = tiles[0], tiles[-1] + 1
                act.activation(V[:, lo:hi, :], KV[:, lo:hi, 1, :], ACT.Copy).then_inc(sems["values_moved"], 1)
                if 0 in tiles:
                    for g in range(PAIRS):
                        copy_out(QT[:, g, :], take()[:, 0:T], scale=float(E) ** -0.5)
                for g in range(PAIRS):
                    copy_out(KT[:, g, columns(tiles)], take()[:, columns(tiles)])
                units(tiles)
                project(tiles)

            def taylor_attention():
                layer_norm()
                copy_out(xT[3][0:C, :], take()[0:C, 0:T])
                need("var_ready")
                act.activation(nrm[:, :, :], nsq[:, :, :], ACT.Sqrt).then_inc(sems["std_ready"], 1)
                for i in range(NT):
                    for half in range(2):
                        copy_out(phi_qT[:, i, half * 4 * TP:(half + 1) * 4 * TP], take()[0:PHI, 0:4 * TP])
                copy_out(xT[4][0:C, :], take()[0:C, 0:T])

            def experts():
                layer_norm()
                copy_out(xT[3][0:C, :], take()[0:C, 0:T])
                for e in range(8):
                    copy_out(hidden[:, e, :], take()[:, 0:T], ACT.Relu)
                exp_of(lexp[:, :], ldiff[:, :])
                for e in range(8, NEXP):
                    copy_out(hidden[:, e, :], take()[:, 0:T], ACT.Relu)
                copy_out(gatesT[:, :], take()[0:NEXP, 0:T])
                layer_norm()

            def carry():
                act.activation(xT[2][0:C, :], xT[1][0:C, :], ACT.Copy)

            def start():
                act.wait_ge(keys_folded, 1)
                for half in range(2):
                    act.activation(Wpk[:, half * 512:(half + 1) * 512], act_bank[half][0:C, :],
                                   ACT.Copy).then_inc(keys_folded, 1)
                act.wait_ge(dve_consts, N_DVE_CONST)
                conv_stage()
                attention0((0,))
                key_scores((0,))
                key_exp()
                units((1, 2))
                project((1, 2))
                key_scores((1, 2))
                key_exp()
                key_exp()

            def iteration(front, back):
                begin()
                if back:
                    ffn_attention()
                carry()
                if front:
                    conv_stage()
                    attention0()
                    key_scores()
                    key_exp()
                if back:
                    taylor_attention()
                    experts()
                if front:
                    key_exp()
                    key_exp()

            def finish():
                begin()
                ffn_attention((0, 1))
                ffn_attention((2,))
                taylor_attention()
                experts()

            run(t, act, start, iteration, finish)

        @block.vector
        def _(dve):
            t = Tally()
            base = [0]
            steps = [0]

            def step(ins):
                ins.then_inc(dve_step, 1)
                steps[0] += 1
                return steps[0]

            def after(k=None):
                dve.wait_ge(dve_step, steps[0] if k is None else k)

            def begin():
                base[0] = t.n.get("dve_filled", 0)

            def end():
                after()
                dve.sem_clear(dve_step)
                steps[0] = 0

            def take():
                k = t.n.get("dve_filled", 0)
                t.raised("dve_filled")
                dve.wait_ge(dve_filled, t.value("dve_filled"))
                return dve_bank[(k - base[0]) % BANKS]

            def drained():
                after()
                dve.sem_inc(dve_drained, 1)

            def signal(name):
                after()
                dve.sem_inc(sems[name], 1)

            def need(name):
                t.raised(name)
                dve.wait_ge(sems[name], t.value(name))

            def layer_stats(src, tiles=ALL):
                for i in tiles:
                    step(dve.bn_stats(bstat[:, i, :], src[:, i, :]))
                for i in tiles:
                    after(steps[0] - len(tiles) + 1)
                    step(dve.bn_aggr(bagg[:, i, :], bstat[:, i, :]))
                signal("var_ready")
                need("std_ready")
                lo, hi = tiles[0], tiles[-1] + 1
                step(dve.reciprocal(rstd[:, lo:hi], std[:, lo:hi]))
                after()

            def layer_norm(src, dst, tiles=ALL):
                layer_stats(src, tiles)
                for i in tiles:
                    step(dve.tensor_scalar(dst[:, i, :], src[:, i, :], bagg[:, i, 0:1], rstd[:, i:i + 1],
                                           ALU.subtract, ALU.mult))
                signal("xn_ready")

            def softmax_units(strict, lots, tiles, scores_bank):
                for u in range(len(tiles) * H + 3):
                    if u < len(tiles) * H:
                        tile = tiles[u // H]
                        t.raised("act_filled")
                        dve.wait_ge(act_filled, t.value("act_filled"))
                        if u >= 1:
                            t.raised("act_filled")
                        dve.tensor_reduce(negmax[:, u % 4:u % 4 + 1], scores_bank(u)[0:TP, 0:(tile + 1) * TP],
                                          AX.X, ALU.max, negate=True).then_inc(sems["max_ready"], 1)
                        t.raised("max_ready")
                        sum_quarters(lots(u))
                    if u >= H + 2 and (u - 2) % H == 0:
                        tile = tiles[(u - 2) // H - 1]
                        b = take()
                        step(dve.reciprocal(rsum[:, tile, :], sums[:, tile, :]))
                        after()
                        if strict and tile == 0:
                            step(dve.tensor_scalar(rsum[:, 0, :], rsum[:, 0, :], row_live[:, 0:1], None, ALU.mult))
                            after()
                        step(dve.tensor_tensor(
                            O[:, tile, :].rearrange("p (h e) -> p h e", h=H),
                            b[0:TP, :].rearrange("p (h e) -> p h e", h=H),
                            rsum[:, tile, :].unsqueeze(2).broadcast_to([TP, H, E]), ALU.mult))
                        drained()
                        dve.sem_inc(sems["o_ready"], 1)
                t.raised("act_filled")

            def add_projection(h, tiles=ALL):
                for _ in tiles:
                    t.raised("act_filled")
                for i in tiles:
                    b = take()
                    step(dve.tensor_tensor(h[:, i, :], h[:, i, :], b[0:TP, 0:C], ALU.add))
                    drained()

            def attention0(lots, fill=0, first=ALL):
                layer_norm(h_front, xn)
                sum_quarters(fill)
                for _ in range(1 + 2 * PAIRS + NT):
                    t.raised("act_filled")
                run_units(True, lots, first)
                add_projection(h_front, first)

            def run_units(strict, lots, tiles=ALL):
                first = t.n["act_filled"] - act_base[0]
                softmax_units(strict, lots, tiles, lambda u: act_bank[(first + (2 * u - 1 if u else 0)) % BANKS])

            act_base = [0]

            def conv_stage():
                t.raised("x_loaded")
                dve.wait_ge(x_loaded, t.value("x_loaded") * 16)
                step(dve.tensor_scalar(conv[:, :], xpad[:, 0:2 * T:2], taps_w[:, 0:1], chan[:, 0:1],
                                       ALU.mult, ALU.add))
                for k in range(1, TAPS):
                    after()
                    step(dve.scalar_tensor_tensor(conv[:, :], xpad[:, k:k + 2 * T:2], taps_w[:, k:k + 1],
                                                  conv[:, :], ALU.mult, ALU.add))
                signal("taps_done")
                step(dve.bn_stats(cstat[:, :], conv[:, :]))
                after()
                step(dve.bn_aggr(cmom[:, :], cstat[:, :]))
                after()
                step(dve.scalar_tensor_tensor(cmom[:, 1:2], cmom[:, 0:1], cmom[:, 0:1], cmom[:, 1:2],
                                              ALU.mult, ALU.add))
                signal("conv_ready")
                b = take()
                step(dve.tensor_copy(call[:, 0:2], b[0:C, 0:2]))
                drained()
                step(dve.tensor_scalar(call[:, 4:5], call[:, 0:1], -1.0, None, ALU.mult))
                after()
                step(dve.scalar_tensor_tensor(call[:, 2:3], call[:, 4:5], call[:, 0:1], call[:, 1:2],
                                              ALU.mult, ALU.add))
                signal("var_ready")
                need("std_ready")
                step(dve.reciprocal(call[:, 5:6], call[:, 3:4]))
                after()
                step(dve.tensor_tensor(call[:, 6:7], call[:, 5:6], chan[:, 1:2], ALU.mult))
                after()
                step(dve.scalar_tensor_tensor(call[:, 7:8], call[:, 4:5], call[:, 6:7], chan[:, 2:3],
                                              ALU.mult, ALU.add))
                after()
                step(dve.tensor_scalar(conv[:, :], conv[:, :], call[:, 6:7], call[:, 7:8], ALU.mult, ALU.add))
                after()
                step(dve.tensor_scalar(conv_neg[:, :], conv[:, :], 0.0, chan[:, 3:4], ALU.min, ALU.mult))
                after()
                step(dve.scalar_tensor_tensor(conv[:, :], conv[:, :], 0.0, conv_neg[:, :], ALU.max, ALU.add))
                signal("conv_ready")
                b = take()
                step(dve.tensor_copy(h_front[:, :, :], b[0:TP, 0:NT * C].rearrange("p (t c) -> p t c", t=NT)))
                drained()

            def top16(count, best_of, at_of, src):
                for lot in range(2):
                    lo, hi = lot * 8, lot * 8 + 8
                    first = steps[0]
                    for g in range(count):
                        if lot:
                            after(first - count + 1 + g)
                        step(dve.max(best_of[:, g, lo:hi], src(g)))
                    for g in range(count):
                        after(first + 1 + g)
                        step(dve.max_index(at_of[:, g, lo:hi], best_of[:, g, lo:hi], src(g)))
                    if lot == 0:
                        for g in range(count):
                            step(dve.match_replace(src(g), best_of[:, g, lo:hi], src(g), -3.0e38))

            def key_norm(tiles=ALL):
                layer_norm(h_front, xn, tiles)
                t.raised("act_filled")
                for tile in tiles:
                    t.raised("act_filled")
                    t.raised("act_filled")
                    scored[tile] = t.n["act_filled"]

            def keys(tile):
                dve.wait_ge(act_drained, t.value("act_filled", scored[tile]))
                dve.sem_inc(dve_step, 1)
                steps[0] += 1
                top16(GROUPS, top, top_at, lambda g: scores[:, tile, g * NKEYS:(g + 1) * NKEYS])
                after()
                step(dve.tensor_copy(top_key[:, 0:H, :], top_at[:, 0:H, :]))
                step(dve.tensor_scalar(top_key[:, H:, :], top_at[:, H:, :], float(NKEYS), -float(KEY_BIAS),
                                       ALU.mult, ALU.add))
                after()
                at, i = 0, 0
                while i < TOPK:
                    n = CAND[i]
                    m = CAND.count(n)
                    for dst, src in ((cand[:, :, at:at + m * n].rearrange("p h (i j) -> p h i j", i=m), top),
                                     (cand_key[:, at:at + m * n, :].rearrange("p (i j) h -> p h i j", i=m), top_key)):
                        step(dve.tensor_tensor(
                            dst, src[:, 0:H, i:i + m].unsqueeze(3).broadcast_to([TP, H, m, n]),
                            src[:, H:, 0:n].unsqueeze(2).broadcast_to([TP, H, m, n]), ALU.add))
                    at, i = at + m * n, i + m
                assert at == NCAND
                after()
                top16(H, best, best_at, lambda h: cand[:, h, :])
                after()
                step(dve.tensor_copy(best_pos[:, :, :], best_at[:, :, :].rearrange("p h k -> p k h")))
                step(dve.tensor_tensor(below[:, :, :], best[:, :, :],
                                       best[:, :, 0:1].broadcast_to([TP, H, TOPK]), ALU.subtract))
                signal("exp_in")
                flat = onehot.rearrange("p c k h -> p c (k h)")
                step(dve.tensor_tensor(onehot, iota_cand[:, :, :].unsqueeze(2).broadcast_to([TP, NCAND, TOPK, H]),
                                       best_pos[:, :, :].unsqueeze(1).broadcast_to([TP, NCAND, TOPK, H]),
                                       ALU.is_equal))
                after()
                step(dve.tensor_tensor(onehot, onehot, cand_key[:, :, :].unsqueeze(2)
                                       .broadcast_to([TP, NCAND, TOPK, H]), ALU.mult))
                n = NCAND
                while n > 1:
                    after()
                    half = n // 2
                    step(dve.tensor_tensor(flat[:, 0:half, :], flat[:, 0:half, :], flat[:, n - half:n, :], ALU.add))
                    n -= half
                after()
                step(dve.tensor_tensor(index[0:TP, tile, :].rearrange("p (h k) -> p h k", h=H),
                                       onehot[:, 0, :, :].rearrange("p k h -> p h k"),
                                       head_offset[:, :].rearrange("p (h k) -> p h k", h=H), ALU.add))
                need("exp_out")
                step(dve.tensor_reduce(esum[:, :], expd[:, :, :], AX.X, ALU.add))
                after()
                step(dve.reciprocal(esum[:, :], esum[:, :]))
                after()
                step(dve.tensor_tensor(weight[:, tile, :, :], expd[:, :, :],
                                       esum[:, :].unsqueeze(2).broadcast_to([TP, H, TOPK]), ALU.mult))
                signal("indices_ready")

            scored = {}

            summed = [0]

            def sum_quarters(count):
                for _ in range(count):
                    (tile, h), part = divmod(summed[0] // 4, H), summed[0] % 4
                    n = t.n.get("rows_used", 0)
                    slot = n % RING
                    kv = KV[:, tile, :, h * E:(h + 1) * E]
                    if part == 0:
                        arrived = 16 * TOPK * (n // RING + 1)
                        if t.turn is not None:
                            arrived = t.turn * (16 * TOPK * NT * H // RING) + arrived
                        dve.wait_ge(landed[slot], arrived)
                    for k in range(4 * part, 4 * part + 4):
                        row = rows[0:TP, slot, k, :].rearrange("p (a e) -> p a e", a=2)
                        w = weight[:, tile, h, k:k + 1]
                        acc = odd[:, :, :] if k % 2 else kv
                        if k < 2:
                            if k == 1:
                                after(steps[0] - 1)
                            step(dve.tensor_scalar(acc, row, w, None, ALU.mult))
                        else:
                            after(steps[0] - 1)
                            step(dve.scalar_tensor_tensor(acc, row, w, acc, ALU.mult, ALU.add))
                    summed[0] += 1
                    if part == 3:
                        signal("rows_used")
                        t.raised("rows_used")
                        step(dve.tensor_tensor(kv, kv, odd[:, :, :], ALU.add))
                        if (h + 1) % H == 0:
                            signal("kv_ready")

            def sum_upto(groups):
                sum_quarters(max(4 * groups - summed[0], 0))

            def ffn_attention(lots, tiles=ALL):
                for _ in range(PAIRS * (2 if 0 in tiles else 1)):
                    t.raised("act_filled")
                dve.wait_ge(act_filled, t.value("act_filled"))
                need("values_moved")
                run_units(False, lots, tiles)
                add_projection(h_back, tiles)

            def taylor_attention(fill=0):
                layer_norm(h_back, xn)
                t.raised("act_filled")
                sum_quarters(fill)
                for i in range(NT):
                    b = take()
                    step(dve.tensor_copy(QK[:, i, :, :].rearrange("p h d -> p (h d)"), b[0:TP, 0:2 * C]))
                    step(dve.tensor_copy(V1[:, i, :, 1:], b[0:TP, 2 * C:3 * C].rearrange("p (h d) -> p h d", h=H)))
                    drained()
                qk = QK[:, :, :, :].rearrange("p t h d -> p (t h d)")
                step(dve.tensor_tensor(QKsq[:, :, :, :].rearrange("p t h d -> p (t h d)"), qk, qk, ALU.mult))
                after()
                flat = nsq[:, :, :].rearrange("p t h -> p (t h)")
                step(dve.tensor_reduce(flat, QKsq[:, :, :, :].rearrange("p t h d -> p (t h) d"), AX.X, ALU.add))
                after()
                step(dve.tensor_tensor(nsq[:, :, :], nsq[:, :, :],
                                       norm_in[:, :].unsqueeze(1).broadcast_to([TP, NT, 2 * H]), ALU.mult))
                signal("var_ready")
                need("std_ready")
                step(dve.tensor_scalar(nrm[:, :, :], nrm[:, :, :], EPS_NORM, None, ALU.max))
                after()
                step(dve.reciprocal(nrm[:, :, :], nrm[:, :, :]))
                after()
                step(dve.tensor_tensor(nrm[:, :, :], nrm[:, :, :],
                                       norm_out[:, :].unsqueeze(1).broadcast_to([TP, NT, 2 * H]), ALU.mult))
                after()
                flat = QK[:, :, :, :].rearrange("p t h d -> p (t h) d")
                step(dve.tensor_tensor(flat, flat, nrm[:, :, :].rearrange("p t h -> p (t h)").unsqueeze(2)
                                       .broadcast_to([TP, NT * 2 * H, D1]), ALU.mult))
                after()
                for first, phi in ((H, phi_k), (0, phi_q)):
                    step(dve.memset(phi[:, :, :, PHI - 1:], 1.0))
                    for i in range(NT):
                        v = QK[:, i, first:first + H, :]
                        step(dve.tensor_tensor(
                            phi[:, i, :, 0:D1 * D1].rearrange("p h (a b) -> p h a b", a=D1),
                            v.unsqueeze(3).broadcast_to([TP, H, D1, D1]),
                            v.unsqueeze(2).broadcast_to([TP, H, D1, D1]), ALU.mult))
                        step(dve.tensor_copy(phi[:, i, :, D1 * D1:D1 * D1 + D1], v))
                signal("phi_ready")
                sum_quarters(fill)
                b = take()
                step(dve.tensor_scalar(KVM[:, :], b[0:PHI, 0:H * (D1 + 1)], phi_coef[0:PHI, 0:1], None, ALU.mult))
                drained()
                dve.sem_inc(sems["kvm_ready"], 1)
                for _ in range(2 * NT):
                    t.raised("act_filled")
                for i in range(NT):
                    b = take()
                    y = b[0:TP, 0:H * (D1 + 1)].rearrange("p (h d) -> p h d", h=H)
                    step(dve.reciprocal(rden[:, i, :], y[:, :, 0]))
                    after()
                    step(dve.tensor_tensor(Y[:, i, :].rearrange("p (h d) -> p h d", h=H), y[:, :, 1:],
                                           rden[:, i, :].unsqueeze(2).broadcast_to([TP, H, D1]), ALU.mult))
                    drained()
                signal("y_ready")
                sum_quarters(fill)
                t.raised("act_filled")
                b = take()
                step(dve.tensor_tensor(h_back[:, :, :], h_back[:, :, :],
                                       b[0:TP, 0:NT * C].rearrange("p (t c) -> p t c", t=NT), ALU.add))
                drained()

            def experts(fill=0, more=0):
                layer_norm(h_back, xn_moe)
                t.raised("act_filled")
                sum_quarters(fill)
                b = take()
                step(dve.tensor_copy(logits[:, :, :], b[0:TP, 0:NT * NEXP].rearrange("p (t e) -> p t e", t=NT)))
                drained()
                for i in range(NT):
                    step(dve.max(lead[:, i, :], logits[:, i, :]))
                for i in range(NT):
                    after(steps[0] - NT + 1)
                    step(dve.max_index(lead_at[:, i, :], lead[:, i, :], logits[:, i, :]))
                after()
                step(dve.tensor_copy(lead_pos[:, :, :], lead_at[:, :, :]))
                step(dve.tensor_tensor(ldiff[:, :], lead[:, :, 1], lead[:, :, 0], ALU.subtract))
                signal("exp_in")
                need("exp_out")
                step(dve.tensor_scalar(gate1[:, :], lexp[:, :], 1.0, None, ALU.add))
                after()
                step(dve.reciprocal(gate1[:, :], gate1[:, :]))
                after()
                step(dve.tensor_tensor(gate2[:, :], lexp[:, :], gate1[:, :], ALU.mult))
                after()
                for i in range(NT):
                    for k, w, dst in ((0, gate1, gates), (1, gate2, gates2)):
                        step(dve.tensor_scalar(dst[:, i, :], iota[:, 0:NEXP], lead_pos[:, i, k:k + 1], w[:, i:i + 1],
                                               ALU.is_equal, ALU.mult))
                after()
                step(dve.tensor_tensor(gates[:, :, :], gates[:, :, :], gates2[:, :, :], ALU.add))
                signal("gates_ready")
                sum_quarters(more)
                for _ in range(NEXP + 1):
                    t.raised("act_filled")
                for i in range(NT):
                    for half in range(2):
                        b = take()
                        step(dve.tensor_tensor(
                            weighed[:, half * 8:half * 8 + 8, :], b[0:TP, :].rearrange("p (e c) -> p e c", e=8),
                            gates[:, i, half * 8:half * 8 + 8].unsqueeze(2).broadcast_to([TP, 8, C]), ALU.mult))
                        drained()
                    step(dve.tensor_reduce(moe[:, i, :], weighed[:, :, :].rearrange("p e c -> p c e"), AX.X, ALU.add))
                    after()
                b = take()
                step(dve.tensor_tensor(moe[:, :, :], moe[:, :, :],
                                       b[0:TP, 0:NT * C].rearrange("p (t c) -> p t c", t=NT), ALU.add))
                drained()
                step(dve.tensor_tensor(moe[:, :, :], moe[:, :, :], xn_moe[:, :, :], ALU.add))
                after()
                layer_stats(moe)
                for i in range(NT):
                    step(dve.tensor_scalar(moe[:, i, :], moe[:, i, :], bagg[:, i, 0:1], rstd[:, i:i + 1],
                                           ALU.subtract, ALU.mult))
                after()
                step(dve.tensor_tensor(moe[:, :, :], moe[:, :, :],
                                       Gamma1[:, :].unsqueeze(1).broadcast_to([TP, NT, C]), ALU.mult))
                after()
                step(dve.tensor_tensor(moe[:, :, :], moe[:, :, :],
                                       Beta1[:, :].unsqueeze(1).broadcast_to([TP, NT, C]), ALU.add))
                after()
                stored = t.n.get("out_ready", 0)
                dve.wait_ge(out_stored, (t.value("out_ready", stored) + 1) * 16)
                step(dve.tensor_tensor(outb[:, :, :], h_back[:, :, :], moe[:, :, :], ALU.add))
                signal("out_ready")
                t.raised("out_ready")

            def move(dst, src):
                step(dve.tensor_copy(dst[:, :, :], src[:, :, :]))
                after()

            def start():
                dve.wait_ge(weights_loaded, 16 * n_loads)
                dve.wait_ge(consts_made, N_CONST)
                made = [0]

                def make(ins):
                    ins.then_inc(dve_consts, 1)
                    made[0] += 1

                for i in (0, 3, 4):
                    make(dve.memset(xT[i][C:C + 1, :], 1.0))
                make(dve.memset(mean_of_c[:, :], 1.0 / C))
                make(dve.memset(eps_conv[:, :], EPS_CONV))
                make(dve.memset(eps_ln[:, :], EPS_LN))
                make(dve.memset(norm_in[:, 0:H], float(D1) ** 0.5))
                make(dve.memset(norm_in[:, H:], 1.0))
                make(dve.memset(norm_out[:, H:], float(D1) ** 0.25))
                make(dve.memset(V1[:, :, :, 0:1], 1.0))
                make(dve.memset(odd[:, :, :], 0.0))
                assert made[0] == N_DVE_CONST, made
                dve.wait_ge(dve_consts, N_DVE_CONST)
                dve.sem_inc(out_stored, 16)
                conv_stage()
                attention0(lambda u: 0, first=(0,))
                key_norm((0,))
                keys(0)
                run_units(True, lambda u: 0, (1, 2))
                add_projection(h_front, (1, 2))
                key_norm((1, 2))
                keys(1)
                sum_upto(4)
                keys(2)
                dve.wait_ge(late_loaded, 16 * n_late)
                step(dve.tensor_scalar(norm_out[:, 0:H], norm_out[:, 0:H], float(D1) ** 0.5, None, ALU.mult))
                end()

            def iteration(front, back):
                begin()
                act_base[0] = t.n["act_filled"]
                if back:
                    summed[0] = 0
                    move(h_back, h_mid)
                else:
                    sum_upto(6)
                move(h_mid, h_front)
                if back:
                    ffn_attention(lambda u: 1)
                if front:
                    conv_stage()
                    attention0(lambda u: min(u % 3, 1), 6)
                sum_upto(H)
                if front:
                    key_norm()
                    keys(0)
                if back:
                    taylor_attention(4)
                    experts(5, 15)
                sum_upto(2 * H)
                if front:
                    keys(1)
                if front:
                    sum_upto(3 * H)
                    keys(2)
                end()

            def finish():
                begin()
                act_base[0] = t.n["act_filled"]
                move(h_back, h_mid)
                ffn_attention(lambda u: 1, (0, 1))
                sum_upto(3 * H)
                ffn_attention(lambda u: 0, (2,))
                taylor_attention()
                experts()

            run(t, dve, start, iteration, finish)


def kernel(**inputs):
    import numpy as _np
    import concourse.bacc as _bacc
    from concourse import mybir as _mybir
    from concourse.bass_utils import run_bass_kernel_spmd as _run

    g = {k: _np.asarray(v) for k, v in inputs.items()}
    row = lambda a: a.reshape(1, -1)
    col = lambda a: a.reshape(-1, 1)
    arrays = {
        "x": g["x"].transpose(0, 2, 1),
        "conv_w": g["L0_tok_w"][:, 0, :].T,
        "conv_b": col(g["L0_tok_b"]), "gamma0": col(g["L0_tok_gamma"]), "beta0": col(g["L0_tok_beta"]),
        "alpha0": col(g["L0_tok_alpha"]),
        "wq": g["L0_attn_Wq"], "bq": row(g["L0_attn_bq"]), "wk": g["L0_attn_Wk"], "bk": row(g["L0_attn_bk"]),
        "wv": g["L0_attn_Wv"], "bv": row(g["L0_attn_bv"]), "wu": g["L0_attn_Wu"], "bu": row(g["L0_attn_bu"]),
        "wpk_t": g["L0_ffn_Wq_pk"].reshape(64, 16, 32).transpose(2, 1, 0),
        "pk_keys_t": g["L0_ffn_pk_keys"].transpose(3, 0, 2, 1).reshape(32, 16, 64),
        "wq2": g["L0_ffn_Wq"],
        "kv_table": _np.concatenate([g["L0_ffn_keys_table"], g["L0_ffn_values_table"]], axis=1),
        "wo": g["L0_ffn_Wo"],
        "wqkv_t": g["L1_attn_Wqkv"].T, "bqkv": row(g["L1_attn_bqkv"]),
        "wproj_t": g["L1_attn_Wproj"].T, "bproj": row(g["L1_attn_bproj"]),
        "temperature": row(g["L1_attn_temperature"]),
        "gate_w": g["L1_ffn_gate_w"], "gate_b": row(g["L1_ffn_gate_b"]),
        "w1": g["L1_ffn_w1"], "b1": g["L1_ffn_b1"], "w2": g["L1_ffn_w2"], "b2": g["L1_ffn_b2"],
        "gamma1": row(g["L1_ffn_gamma"]), "beta1": row(g["L1_ffn_beta"]),
    }
    nc = _bacc.Bacc("TRN2", target_bir_lowering=False, num_devices=1)
    args, feeds = [], {}
    for name, a in arrays.items():
        a = _np.ascontiguousarray(a)
        feeds[f"in_{name}"] = a
        args.append(nc.dram_tensor(f"in_{name}", a.shape, _mybir.dt.from_np(a.dtype), kind="ExternalInput").ap())
    o = nc.dram_tensor("out_0", (BATCH, T, C), F32, kind="ExternalOutput").ap()
    build(nc, *args, o)
    r = _run(nc, [feeds], core_ids=[0])
    return r.results[0]["out_0"]
```
